# Optimizing a Trainium2 kernel written in Bass

```python
import numpy as np
import jax
import jax.numpy as jnp

def _softmax(x, axis=-1):
    return jax.nn.softmax(x, axis=axis)

def _gelu(x):
    return jax.nn.gelu(x, approximate=True)

def _silu(x):
    return jax.nn.silu(x)

def _sigmoid(x):
    return jax.nn.sigmoid(x)

def _layernorm(x, axis=-1, eps=1e-05):
    m = jnp.mean(x, axis=axis, keepdims=True)
    v = jnp.var(x, axis=axis, keepdims=True)
    return (x - m) / jnp.sqrt(v + eps)

def _scatter_add(tgt, idx, src, axis=0):
    return tgt.at[idx].add(src)

def _segment_sum(src, seg, n):
    return jax.ops.segment_sum(src, seg, n)
kernel_name = 'mk_adj_resnorm_d2_adj_r2_a623fd'

def setup_inputs(seed: int=0):
    np.random.seed(seed)
    _w = jnp.asarray

    def _rec_inputs():
        import jax
        import jax.numpy as jnp
        _gk = jax.random.key(seed)
        x = -0.000929 + 1 * jax.random.normal(jax.random.fold_in(_gk, 1), (8192, 64), jnp.float32)
        _a = jax.random.bernoulli(jax.random.fold_in(_gk, 2), 0.000488281, (8192, 8192))
        _a = jnp.logical_or(_a, jnp.swapaxes(_a, -1, -2))
        _a = jnp.logical_or(_a, jnp.eye(8192, dtype=bool))
        _af = _a.astype(jnp.float32)
        adj = _af
        return (x, adj)
    x, adj = _rec_inputs()

    def _L0_gnn_setup():
        import jax, jax.numpy as jnp
        import numpy as np
        N, D_IN, D_OUT = (8192, 64, 64)
        AVG_DEG = 32.0
        L2_EPS = 1e-12
        key = jax.random.key(seed)
        kx, ka, kw, kb = jax.random.split(key, 4)
        X = jax.random.normal(kx, (N, D_IN), dtype=jnp.float32)
        adj = (jax.random.uniform(ka, (N, N)) < AVG_DEG / N).astype(jnp.float32)
        bound = 1.0 / np.sqrt(2 * D_IN)
        W = jax.random.uniform(kw, (2 * D_IN, D_OUT), dtype=jnp.float32, minval=-bound, maxval=bound)
        b = jax.random.uniform(kb, (D_OUT,), dtype=jnp.float32, minval=-bound, maxval=bound)
        return {'X': X, 'adj': adj, 'W': W, 'b': b}
    _L0_gnn_all = _L0_gnn_setup()
    _L0_gnn_in = {k: v for k, v in _L0_gnn_all.items() if k in ('W', 'b')}
    del _L0_gnn_all

    def _L1_gnn_setup():
        import jax, jax.numpy as jnp
        import numpy as np
        N = 8192
        F = 64
        O = 64
        key = jax.random.key(seed)
        k1, k2, k3 = jax.random.split(key, 3)
        features = jax.random.normal(k1, (N, F), dtype=jnp.float32)
        adj = jax.random.uniform(k2, (N, N), dtype=jnp.float32)
        W = jax.random.normal(k3, (O, 2 * F), dtype=jnp.float32)
        return {'features': features, 'adj': adj, 'W': W}
    _L1_gnn_all = _L1_gnn_setup()
    _L1_gnn_in = {k: v for k, v in _L1_gnn_all.items() if k in ('W',)}
    del _L1_gnn_all
    return {'x': x, 'adj': adj, 'L0_gnn_W': _L0_gnn_in['W'], 'L0_gnn_b': _L0_gnn_in['b'], 'L1_gnn_W': _L1_gnn_in['W']}

def reference(x, adj, L0_gnn_W, L0_gnn_b, L1_gnn_W):
    import jax
    import jax.numpy as jnp

    def _L0_gnn_ref(X, adj, W, b):
        import jax, jax.numpy as jnp
        import numpy as np
        N, D_IN, D_OUT = (8192, 64, 64)
        AVG_DEG = 32.0
        L2_EPS = 1e-12
        deg = jnp.clip(jnp.sum(adj, axis=1, keepdims=True) + 1.0, 1.0, None)
        h_neigh = (adj @ X + X) / deg
        concat = jnp.concatenate([X, h_neigh], axis=1)
        z = concat @ W + b
        out = jax.nn.relu(z)
        norm = jnp.linalg.norm(out, axis=1, keepdims=True)
        return out / jnp.maximum(norm, L2_EPS)

    def _L1_gnn_ref(features, adj, W):
        import jax, jax.numpy as jnp
        import numpy as np
        N = 8192
        F = 64
        O = 64
        deg = jnp.sum(adj, axis=1, keepdims=True)
        neigh = adj @ features / (deg + 1.0)
        data = jnp.concatenate([features, neigh], axis=-1)
        return data @ W.T
    x = _layernorm(x + _L0_gnn_ref(x, adj, L0_gnn_W, L0_gnn_b), axis=-1)
    x = _layernorm(x + _L1_gnn_ref(x, adj, L1_gnn_W), axis=-1)
    return x

_drawn_inputs = setup_inputs


def setup_inputs(seed=0):
    import zlib

    import numpy as np

    out = dict(_drawn_inputs(seed))
    spreads = {}
    factors = {'L0_gnn_b': 2.874}
    for name, (base, spread) in spreads.items():
        noise = np.random.default_rng([zlib.crc32(name.encode()), seed]).standard_normal(out[name].shape)
        drawn = base * np.exp(spread * noise) if base else spread * noise
        out[name] = jnp.asarray(drawn.astype(out[name].dtype))
    for name, factor in factors.items():
        out[name] = (out[name] * factor).astype(out[name].dtype)
    return out
```

```python
from contextlib import ExitStack

import concourse.bass as bass
from concourse import mybir

F32 = mybir.dt.float32
BF16 = mybir.dt.bfloat16
FP8 = mybir.dt.float8e4
U8 = mybir.dt.uint8
U32 = mybir.dt.uint32
I32 = mybir.dt.int32
ALU = mybir.AluOpType
ACT = mybir.ActivationFunctionType
AX_X = mybir.AxisListType.X

N = 8192
F = 64
P = 128
NB = N // P
CH = 2048
NC = N // CH
CB = CH // P
BR = 4
NBATCH = NB // BR
NQ = 4
QR = NB // NQ
QB = QR // BR
PARTS = 3 * F
ZW = 2 * PARTS + 1
ZP = ZW + 1
BIT = 0x40
BIT4 = 0x40404040
EPS = 1e-5


def low(q):
    return max(0, QR * q - BR)


def plane_base(q):
    return sum(2 * (NB - low(s)) for s in range(q))


class Links:

    def __init__(self, eng, sem):
        self.eng, self.sem, self.base, self.n = eng, sem, 0, 0

    def __call__(self, ins, settle=None):
        self.n += 1
        ins.then_inc(self.sem, 1)
        value = self.base + self.n
        if settle and not isinstance(value, int):
            self.eng.compute_val(value)
            settle(self.eng)
        self.eng.wait_ge(self.sem, value)

    def at(self, base):
        self.base, self.n = base, 0


def gnn_kernel(nc, x, adj, w0, b0, w1, out):
    ctx = ExitStack()
    with ctx:
        def sb(name, shape, dt):
            return ctx.enter_context(nc.sbuf_tensor(name, shape, dt))

        def sem(name):
            return ctx.enter_context(nc.semaphore(name))

        a_in = sb("a_in", [P, NC, CH], F32)
        t_sb = sb("t_sb", [P, 2, NB, P], FP8)
        packed = sb("packed", [P, plane_base(NQ) * P // 4], U32)
        Z = sb("Z", [P, NB, ZP], BF16)
        lower = sb("lower", [P, NB, F], F32)
        xh = sb("xh", [P, NB, F], F32)
        agg = sb("agg", [P, 2, BR, ZW], F32)
        ok_out = sb("ok_out", [P, CH], U8)
        ok = sb("ok", [P, 8 * NC], F32)
        ok_min = sb("ok_min", [P, 8 * NC], F32)
        ok_one = sb("ok_one", [P, 2], F32)
        bad_i = sb("bad_i", [1, 1], I32)
        split_v = lower[:, 0:CB, :]
        split_p = lower[:, CB:2 * CB, :]
        ident_bf = sb("ident_bf", [P, P], BF16)
        ident = sb("ident", [P, P], F32)
        ones_f = sb("ones_f", [P, P], F32)
        w0_sb = sb("w0_sb", [P, F], F32)
        w1_raw = sb("w1_raw", [F, P], F32)
        w1_sb = sb("w1_sb", [P, F], F32)
        b0_sb = sb("b0_sb", [1, F], F32)
        part_sum = sb("part_sum", [P, BR, F], F32)
        nsum = sb("nsum", [P, BR, F], F32)
        cat = sb("cat", [P, BR, 2 * F], F32)
        cat_t = sb("cat_t", [P, BR, P], F32)
        z_sb = sb("z_sb", [P, BR, F], F32)
        y_sb = sb("y_sb", [P, BR, F], F32)
        sq_sb = sb("sq_sb", [P, BR, F], F32)
        hn_sb = sb("hn_sb", [P, BR, F], F32)
        rest = sb("rest", [P, BR, F], F32)
        o_sb = sb("o_sb", [P, 2, BR, F], F32)
        small = sb("small", [P, 8, BR], F32)
        minus_half = sb("minus_half", [P, BR], F32)
        rdeg2 = sb("rdeg2", [P, NB], F32)

        t_ps = [ctx.enter_context(nc.psum_tensor(f"t_ps{i}", [P, CB, P], BF16)) for i in range(2)]
        s_ps = [ctx.enter_context(nc.psum_tensor(f"s_ps{i}", [P, 512], F32)) for i in range(2)]
        c_ps = ctx.enter_context(nc.psum_tensor("c_ps", [P, BR, P], F32))
        z_ps = ctx.enter_context(nc.psum_tensor("z_ps", [P, 512], F32))

        s_in = [sem(f"s_in{c}") for c in range(NC)]
        s_x = [sem(f"s_x{q}") for q in range(NQ)]
        s_w = sem("s_w")
        s_identbf = sem("s_identbf")
        s_w1t = sem("s_w1t")
        s_w1 = sem("s_w1")
        s_xv = sem("s_xv")
        s_xp = sem("s_xp")
        s_tps = sem("s_tps")
        s_tsb = sem("s_tsb")
        s_chk = sem("s_chk")
        s_pack = sem("s_pack")
        s_sum = sem("s_sum")
        s_agg = sem("s_agg")
        s_low = sem("s_low")
        s_feat = sem("s_feat")
        s_mean = sem("s_mean")
        s_catps = sem("s_catps")
        s_catt = sem("s_catt")
        s_zps = sem("s_zps")
        s_z = sem("s_z")
        s_var = sem("s_var")
        s_root = sem("s_root")
        s_hn = sem("s_hn")
        s_h = sem("s_h")
        s_unp = sem("s_unp")
        s_o = sem("s_o")
        s_out = [sem(f"s_out{i}") for i in range(2)]
        s_bad = sem("s_bad")
        s_badps = sem("s_badps")
        s_flag = sem("s_flag")
        s_dve = sem("s_dve")
        s_pool = sem("s_pool")

        out_v = out.rearrange("(e k p) f -> e p k f", k=BR, p=P)
        adj_v = adj.rearrange("(n p) c -> n p c", p=P)
        x_v = x.rearrange("(n p) f -> p n f", p=P)

        a_hi = [a_in[:, c, :].bitcast(BF16).rearrange("p (b two) -> p b two", two=2)[:, :, 1]
                for c in range(NC)]

        def words(ap):
            return ap.rearrange("p b i -> p (b i)").bitcast(U32)

        def plane(q, g, gdyn=None):
            width = (NB - low(q)) * P // 4
            base = plane_base(q) * P // 4
            if gdyn is not None:
                return packed[:, bass.ds(gdyn * width + base, width)]
            return packed[:, base + g * width:base + (g + 1) * width]

        def zone(t, b):
            return t[:, bass.ds(b, BR), :]

        def zdeg(rows):
            return rdeg2[:, bass.ds(rows, BR)]

        g_feat = packed[:, 0:NB * (F + 1)].bitcast(F32).rearrange("p (n f) -> p n f", f=F + 1)
        g_agg = packed[:, NB * (F + 1):2 * NB * (F + 1)].bitcast(F32).rearrange("p (n f) -> p n f", f=F + 1)
        g_t = packed[:, 2 * NB * (F + 1):2 * NB * (F + 1) + 2 * BR * P].bitcast(F32).rearrange(
            "p (s b i) -> p s b i", s=2, i=P)
        GQ = NB // BR
        tf_ps = [t[:, 0:2 * BR, :].rearrange("p b i -> p (b i)").bitcast(F32).rearrange("p (b i) -> p b i", i=P)
                 for t in t_ps]
        g_x = sem("g_x")
        g_in = [sem(f"g_in{c}") for c in range(NC)]
        g_tps = sem("g_tps")
        g_tsb = sem("g_tsb")
        g_use = sem("g_use")
        g_took = sem("g_took")
        g_ready = sem("g_ready")
        g_cat = sem("g_cat")
        g_catps = sem("g_catps")
        g_catt = sem("g_catt")
        g_zps = sem("g_zps")
        g_z = sem("g_z")
        g_var = sem("g_var")
        g_root = sem("g_root")
        g_h = sem("g_h")
        g_o = sem("g_o")
        g_out = sem("g_out")
        s_const = sem("s_const")

        def count(eng, value):
            if not isinstance(value, int):
                eng.compute_val(value)
            return value

        def settle(eng):
            eng.wait_ge(s_const, 1)

        def if_bad(eng, general):
            eng.wait_ge(s_flag, 1)
            verdict = eng.value_load(bad_i[0:1, 0:1], min_val=0, max_val=P)
            with eng.If(verdict != 0):
                for i in range(2):
                    eng.wait_ge(s_out[i], 16 * NBATCH // 2)
                general()

        block = ctx.enter_context(nc.Block())

        @block.sync
        def _(sp):
            def load_row(n, first=False):
                for c in range(NC):
                    if not first:
                        sp.wait_ge(s_tps, (n - 1) * NC + c + 1)
                        sp.wait_ge(s_chk, (n - 1) * NC + c + 1)
                    src = adj_v[0, :, c * CH:(c + 1) * CH] if first else \
                        adj_v[bass.ds(n, 1), :, c * CH:(c + 1) * CH].rearrange("a p c -> (a p) c")
                    sp.dma_start(a_in[:, c, :], src).then_inc(s_in[c], 16)

            load_row(0, first=True)
            with sp.Fori(1, NB) as n:
                load_row(n)

            with sp.Fori(0, NBATCH // 2) as e2:
                for i in range(2):
                    e = e2 * 2 + i
                    sp.wait_ge(s_o, e + 1)
                    sp.dma_start(out_v[bass.ds(e, 1), :, :, :].rearrange("a p k f -> (a p) k f"),
                                 o_sb[:, i, :, :]).then_inc(s_out[i], 16)
            for i in range(2):
                sp.wait_ge(s_out[i], 16 * NBATCH // 2)

            def general_sp():
                sp.sem_inc(g_out, 16)
                sp.dma_start(xh[:, :, :], x_v).then_inc(g_x, 16)
                for layer in range(2):
                    with sp.Fori(0, NB) as n:
                        for c in range(NC):
                            sp.wait_ge(g_tps, n * GQ + (layer * NB * GQ + 1))
                            sp.dma_start(a_in[:, c, :], adj_v[bass.ds(n, 1), :, c * CH:(c + 1) * CH]
                                         .rearrange("a p c -> (a p) c")).then_inc(g_in[c], 16)
                with sp.Fori(0, NBATCH) as e:
                    sp.wait_ge(g_o, e + 1)
                    sp.dma_start(out_v[bass.ds(e, 1), :, :, :].rearrange("a p k f -> (a p) k f"),
                                 o_sb[:, 0, :, :]).then_inc(g_out, 16)
                sp.wait_ge(g_out, 16 * NBATCH + 16)
            if_bad(sp, general_sp)

        @block.tensor
        def _(pe):
            def transpose_chunk(n, c):
                pe.wait_ge(s_in[c], 16 * (n + 1))
                t = (n * NC + c)
                if not (isinstance(n, int) and t < 2):
                    pe.wait_ge(s_tsb, t - 1)
                for b in range(CB):
                    last = nc.tensor.transpose(t_ps[c % 2][:, b, :], a_hi[c][:, b * P:(b + 1) * P], ident_bf[:, :])
                last.then_inc(s_tps, 1)

            def sum_chunk(q, n, k, c):
                chunk = count(pe, n * NC + c + 1)
                old = count(pe, n - 1) if c == 0 and not (isinstance(n, int) and n < 2) else None
                settle(pe)
                pe.wait_ge(s_tsb, chunk)
                if q == 0 and isinstance(n, int) and n == 0:
                    if c < 3:
                        pe.wait_ge(s_xv, c + 1)
                    else:
                        pe.wait_ge(s_xp, 1)
                if old is not None:
                    pe.wait_ge(s_agg, old)
                if q > 0 and c == 0 and k == 0:
                    pe.wait_ge(s_h, QB * q - 1)
                for b in range(c * CB, (c + 1) * CB):
                    at = 0 if b < low(q) else PARTS
                    last = nc.tensor.matmul(s_ps[k % 2][:, at:ZW], t_sb[:, k % 2, b, :], Z[:, b, at:ZW],
                                            start=(b == 0), stop=(b == NB - 1))
                if c == NC - 1:
                    last.then_inc(s_sum, 1)

            def transpose_cat(e):
                pe.wait_ge(s_feat, e + 1)
                pe.wait_ge(s_mean, e + 1)
                for k in range(BR):
                    last = nc.tensor.transpose(c_ps[:, k, :], cat[:, k, :], ident[:, :])
                last.then_inc(s_catps, 1)

            def dense_products(w, bias):
                for k in range(BR):
                    last = nc.tensor.matmul(z_ps[:, k * F:(k + 1) * F], cat_t[:, k, :], w[:, :],
                                            start=True, stop=not bias)
                    if bias:
                        last = nc.tensor.matmul(z_ps[:, k * F:(k + 1) * F], ones_f[0:1, :], b0_sb[0:1, :],
                                                start=False, stop=True)
                return last

            def dense(e, w, bias):
                pe.wait_ge(s_catt, e + 1)
                dense_products(w, bias).then_inc(s_zps, 1)

            def body(q, e, first=False):
                chunks = [(k, c) for k in range(BR) for c in range(NC)]
                transpose_chunk(e * BR, 0)
                for i, (k, c) in enumerate(chunks):
                    if i + 1 < len(chunks):
                        k1, c1 = chunks[i + 1]
                        transpose_chunk(e * BR + k1, c1)
                    sum_chunk(q, e * BR + k, k, c)
                    if not first and (k, c) == (1, 1):
                        transpose_cat(e - 1)
                    if not first and (k, c) == (2, 0):
                        dense(e - 1, w0_sb, True)

            def general_pe():
                for t in (g_tps, g_use, g_catps):
                    pe.sem_inc(t, 1)
                for layer in range(2):
                    w, bias = ((w0_sb, True), (w1_sb, False))[layer]

                    def transpose_group(n, g):
                        if g % (GQ // NC) == 0:
                            pe.wait_ge(g_in[g * NC // GQ], n * 16 + (layer * NB + 1) * 16)
                        if g >= 2:
                            pe.wait_ge(g_tsb, n * GQ + (layer * NB * GQ + g))
                        for b in range(BR):
                            col = (g * BR + b) * P
                            last = nc.tensor.transpose(tf_ps[g % 2][:, b, :],
                                                       a_in[:, col // CH, col % CH:col % CH + P], ident[:, :])
                        last.then_inc(g_tps, 1)

                    pe.wait_ge(g_ready, layer + 1)
                    with pe.Fori(0, NB) as n:
                        pe.wait_ge(g_tsb, n * GQ + (layer * NB * GQ + 1))
                        pe.wait_ge(g_took, n + (layer * NB + 1))
                        transpose_group(n, 0)
                        for g in range(GQ):
                            if g + 1 < GQ:
                                transpose_group(n, g + 1)
                            pe.wait_ge(g_tsb, n * GQ + (layer * NB * GQ + g + 2))
                            for b in range(BR):
                                last = nc.tensor.matmul(s_ps[0][:, 0:F + 1], g_t[:, g % 2, b, :],
                                                        g_feat[:, g * BR + b, :],
                                                        start=(g == 0 and b == 0), stop=(g == GQ - 1 and b == BR - 1))
                            last.then_inc(g_use, 1)
                    with pe.Fori(0, NBATCH) as e:
                        b = e + layer * NBATCH
                        pe.wait_ge(g_cat, b * 2 + 2)
                        for k in range(BR):
                            last = nc.tensor.transpose(c_ps[:, k, :], cat[:, k, :], ident[:, :])
                        last.then_inc(g_catps, 1)
                        pe.wait_ge(g_catt, b + 1)
                        dense_products(w, bias).then_inc(g_zps, 1)

            pe.wait_ge(s_const, 1)
            pe.wait_ge(s_identbf, 1)
            pe.wait_ge(s_w, 48)
            nc.tensor.transpose(c_ps[:, 0, 0:F], w1_raw[:, :], ident[0:F, 0:F]).then_inc(s_w1t, 1)
            pe.wait_ge(s_w1, 1)
            body(0, 0, first=True)
            for q in range(NQ):
                with pe.Fori(1 if q == 0 else q * QB, (q + 1) * QB) as e:
                    body(q, e)
            def upper_cols(q, n, k, b0, b1):
                if b0 == low(q):
                    this, old = count(pe, n + 1), count(pe, n + (NB - 1))
                    settle(pe)
                    pe.wait_ge(s_unp, this)
                    pe.wait_ge(s_agg, old)
                for b in range(b0, b1):
                    last = nc.tensor.matmul(s_ps[k % 2][:, 0:PARTS], t_sb[:, k % 2, b, :], Z[:, b, 0:PARTS],
                                            start=(b == low(q)), stop=(b == NB - 1))
                if b1 == NB:
                    last.then_inc(s_sum, 1)

            def upper_body(q, e, first=False):
                for k in range(BR):
                    if not (first and k < 2):
                        upper_cols(q, e * BR + k, k, low(q), NB)
                    if not first and k == 2:
                        transpose_cat(e + NBATCH - 1)
                if not first:
                    dense(e + NBATCH - 1, w1_sb, False)

            pe.wait_ge(s_h, NBATCH - 1)
            upper_cols(0, 0, 0, 0, NB - BR)
            transpose_cat(NBATCH - 1)
            dense(NBATCH - 1, w0_sb, True)
            pe.wait_ge(s_bad, 1)
            nc.tensor.matmul(c_ps[0:1, 0, 0:1], ok_one[:, 1:2], ones_f[:, 0:1], start=True,
                             stop=True).then_inc(s_badps, 1)
            upper_cols(0, 1, 1, 0, NB - BR)
            pe.wait_ge(s_h, NBATCH)
            upper_cols(0, 0, 0, NB - BR, NB)
            upper_cols(0, 1, 1, NB - BR, NB)
            upper_body(0, 0, first=True)
            for q in range(NQ):
                with pe.Fori(1 if q == 0 else q * QB, (q + 1) * QB) as e:
                    upper_body(q, e)
            transpose_cat(2 * NBATCH - 1)
            dense(2 * NBATCH - 1, w1_sb, False)
            if_bad(pe, general_pe)

        @block.scalar
        def _(act):
            for q in range(NQ):
                act.dma_start(xh[:, q * CB:(q + 1) * CB, :], x_v[:, q * CB:(q + 1) * CB, :]).then_inc(s_x[q], 16)
            act.dma_start(w0_sb[:, :], w0[:, :]).then_inc(s_w, 16)
            act.dma_start(w1_raw[:, :], w1[:, :]).then_inc(s_w, 16)
            act.dma_start(b0_sb[0:1, :], b0.unsqueeze(0)).then_inc(s_w, 16)
            act.wait_ge(s_w1t, 1)
            nc.scalar.copy(w1_sb[:, :], c_ps[:, 0, 0:F]).then_inc(s_w1, 1)

            def evacuate(n, k, c):
                chunk = count(act, n * NC + c + 1)
                old = count(act, n - 1) if c == 0 and not (isinstance(n, int) and n < 2) else None
                settle(act)
                act.wait_ge(s_tps, chunk)
                if old is not None:
                    act.wait_ge(s_sum, old)
                    act.wait_ge(s_pack, old)
                nc.scalar.activation(t_sb[:, k % 2, c * CB:(c + 1) * CB, :].rearrange("p b i -> p (b i)"),
                                     t_ps[c % 2][:, :, :].rearrange("p b i -> p (b i)"),
                                     ACT.Copy, scale=2.0, saturate=False).then_inc(s_tsb, 1)

            def take_sums(n, e, slot, k, at, to, free):
                act.wait_ge(s_sum, n + 1)
                if k == 0 and free:
                    act.wait_ge(s_low, e - 1)
                    act.wait_ge(s_mean, e - 1)
                nc.scalar.copy(agg[:, slot, k, at:to], s_ps[k % 2][:, at:to]).then_inc(s_agg, 1)

            def features(e, rows):
                if not (isinstance(e, int) and e == 0):
                    act.wait_ge(s_catps, e)
                nc.scalar.copy(cat[:, :, 0:F], rows).then_inc(s_feat, 1)

            def take_cat(e):
                act.wait_ge(s_catps, e + 1)
                if not (isinstance(e, int) and e == 0):
                    act.wait_ge(s_zps, e)
                nc.scalar.copy(cat_t[:, :, :].rearrange("p k i -> p (k i)"),
                               c_ps[:, :, :].rearrange("p k i -> p (k i)")).then_inc(s_catt, 1)

            def take_z(e, func, read, count):
                act.wait_ge(s_zps, e + 1)
                if not (isinstance(count, int) and count == 0):
                    act.wait_ge(read, count)
                nc.scalar.activation(z_sb[:, :, :].rearrange("p k i -> p (k i)"), z_ps[:, 0:BR * F],
                                     func).then_inc(s_z, 1)

            def body(q, e, par, first=False):
                at = 0 if q else PARTS
                for k in range(BR):
                    for c in range(NC):
                        evacuate(e * BR + k, k, c)
                        if c == 0 and not (first and k == 0):
                            if k == 0:
                                take_sums(e * BR - 1, e - 1, 1 - par, BR - 1, at, ZW, False)
                            else:
                                take_sums(e * BR + k - 1, e, par, k - 1, at, ZW,
                                          not (isinstance(e, int) and e < 2))
                        if first:
                            continue
                        if (k, c) == (0, 1):
                            features(e - 1, zone(xh, (e - 1) * BR))
                        if (k, c) == (1, 3):
                            take_cat(e - 1)
                        if (k, c) == (2, 1):
                            take_z(e - 1, ACT.Relu, s_hn, e - 1)

            def general_act():
                act.sem_inc(g_tsb, 1)
                for layer in range(2):
                    with act.Fori(0, NB) as n:
                        for g in range(GQ):
                            act.wait_ge(g_tps, n * GQ + (layer * NB * GQ + g + 2))
                            if g >= 2:
                                act.wait_ge(g_use, n * GQ + (layer * NB * GQ + g))
                            else:
                                act.wait_ge(g_use, n * GQ + (layer * NB * GQ + 1))
                            nc.scalar.copy(g_t[:, g % 2, :, :], tf_ps[g % 2]).then_inc(g_tsb, 1)
                    with act.Fori(0, NBATCH) as e:
                        b = e + layer * NBATCH
                        act.wait_ge(g_catps, b + 2)
                        nc.scalar.copy(cat_t[:, :, :], c_ps[:, :, :]).then_inc(g_catt, 1)
                        act.wait_ge(g_zps, b + 1)
                        nc.scalar.activation(z_sb[:, :, :].rearrange("p k i -> p (k i)"), z_ps[:, 0:BR * F],
                                             ACT.Copy if layer else ACT.Relu).then_inc(g_z, 1)

            for q in range(NQ):
                if q == 0:
                    for e in range(QB):
                        body(0, e, e % 2, first=(e == 0))
                else:
                    with act.Fori(q * QB // 2, (q + 1) * QB // 2) as e2:
                        for par in range(2):
                            body(q, e2 * 2 + par, par)
            e = NBATCH - 1
            take_sums(NB - 1, e, e % 2, BR - 1, 0, ZW, False)
            features(e, xh[:, e * BR:(e + 1) * BR, :])
            take_cat(e)
            take_z(e, ACT.Relu, s_hn, e)

            def upper_body(e, par, first=False):
                for k in range(BR):
                    take_sums(NB + e * BR + k, NBATCH + e, par, k, 0, PARTS, True)
                    if k == 2:
                        if not first:
                            take_cat(NBATCH + e - 1)
                        features(NBATCH + e, zone(xh, e * BR))
                if not first:
                    if isinstance(e, int) and e == 1:
                        take_z(NBATCH + e - 1, ACT.Copy, s_hn, NBATCH)
                    else:
                        take_z(NBATCH + e - 1, ACT.Copy, s_o, e - 1)

            upper_body(0, 0, first=True)
            upper_body(1, 1)
            with act.Fori(1, NBATCH // 2) as e2:
                for par in range(2):
                    upper_body(e2 * 2 + par, par)
            take_cat(2 * NBATCH - 1)
            take_z(2 * NBATCH - 1, ACT.Copy, s_o, NBATCH - 1)
            if_bad(act, general_act)

        LINKS1 = 5 + 9
        LINKS2 = 6

        @block.vector
        def _(dve):
            link = Links(dve, s_dve)
            bc = lambda t: t.unsqueeze(2).to_broadcast([P, BR, F])

            for t in s_ps:
                link(nc.vector.memset(t[:, 0:PARTS], 0.0))
            dve.wait_ge(s_const, 1)
            nc.vector.tensor_copy(ident_bf[:, :], ident[:, :]).then_inc(s_identbf, 1)
            link(nc.vector.memset(Z[:, :, 2 * PARTS:ZW], 1.0))
            link(nc.vector.memset(ok_min[:, :], float(CH)))
            for q in range(3):
                dve.wait_ge(s_x[q], 16)
                cols = slice(q * CB, (q + 1) * CB)
                hi, mid, lo = (Z[:, cols, PARTS + i * F:PARTS + (i + 1) * F] for i in range(3))
                link(nc.vector.tensor_copy(hi, xh[:, cols, :]))
                link(nc.vector.tensor_tensor(split_v, xh[:, cols, :], hi, ALU.subtract))
                link(nc.vector.tensor_copy(mid, split_v))
                nc.vector.tensor_tensor(lo, split_v, mid, ALU.subtract).then_inc(s_xv, 1)
            dve.wait_ge(s_xv, 3)
            start = link.n

            def check(n, r8, c):
                dve.wait_ge(s_in[c], 16 * (n + 1))
                if not (isinstance(n, int) and n == 0 and c == 0):
                    dve.wait_ge(s_chk, n * NC + c)
                col = ok[:, r8 * NC + c:r8 * NC + c + 1]
                nc.vector.scalar_tensor_tensor(out=ok_out[:, :], in0=a_in[:, c, :], scalar=1.0, in1=a_in[:, c, :],
                                               op0=ALU.is_equal, op1=ALU.is_equal,
                                               accum_out=col).then_inc(s_chk, 1)

            def pack(q, n, r8, g, gdyn):
                dve.wait_ge(s_tsb, (n + 1) * NC)
                if r8:
                    dve.wait_ge(s_pack, n)
                dst = plane(q, g, gdyn)
                src = words(t_sb[:, r8 % 2, low(q):NB, :])
                shift = (ALU.logical_shift_right, 6 - r8) if r8 < 7 else (ALU.logical_shift_left, 1)
                if r8 == 0:
                    ins = nc.vector.tensor_scalar(dst, src, shift[1], None, shift[0])
                else:
                    ins = nc.vector.scalar_tensor_tensor(out=dst, in0=src, scalar=shift[1], in1=dst,
                                                         op0=shift[0], op1=ALU.bitwise_or)
                ins.then_inc(s_pack, 1)

            def mean1_steps(total, deg, rows, scale):
                link(nc.vector.tensor_scalar(small[:, 0, :], deg, scale, 1.0, ALU.mult, ALU.add))
                link(nc.vector.reciprocal(zdeg(rows), small[:, 0, :]))
                link(nc.vector.tensor_scalar(small[:, 1, :], small[:, 0, :], 1.0, None, ALU.max))
                link(nc.vector.reciprocal(small[:, 2, :], small[:, 1, :]))
                link(nc.vector.scalar_tensor_tensor(out=nsum[:, :, :], in0=total, scalar=scale,
                                                    in1=zone(xh, rows), op0=ALU.mult, op1=ALU.add))
                return nc.vector.tensor_tensor(cat[:, :, F:2 * F], nsum[:, :, :], bc(small[:, 2, :]), ALU.mult)

            def mean1(e, par):
                dve.wait_ge(s_low, e + 1)
                dve.wait_ge(s_feat, e + 1)
                deg = agg[:, par, :, ZW - 1:ZW].rearrange("p k o -> p (k o)")
                mean1_steps(part_sum[:, :, :], deg, e * BR, 0.5).then_inc(s_mean, 1)

            def rsqrt_by_pool(ins, done, out_sem, count):
                ins.then_inc(done, 1)
                dve.wait_ge(out_sem, count)

            def norm_stats(done, out_sem, count):
                link(nc.vector.tensor_reduce(small[:, 5, :], y_sb[:, :, :], AX_X, ALU.add))
                link(nc.vector.tensor_scalar(small[:, 5, :], small[:, 5, :], 1.0 / F, None, ALU.mult))
                link(nc.vector.tensor_tensor(y_sb[:, :, :], y_sb[:, :, :], bc(small[:, 5, :]), ALU.subtract))
                link(nc.vector.tensor_tensor(sq_sb[:, :, :], y_sb[:, :, :], y_sb[:, :, :], ALU.mult))
                link(nc.vector.tensor_reduce(small[:, 6, :], sq_sb[:, :, :], AX_X, ALU.add))
                ins = nc.vector.tensor_scalar(small[:, 6, :], small[:, 6, :], 1.0 / F, EPS, ALU.mult, ALU.add)
                rsqrt_by_pool(ins, done, out_sem, count)

            def finish1_steps(rows, done, out_sem, count):
                link(nc.vector.tensor_tensor(sq_sb[:, :, :], z_sb[:, :, :], z_sb[:, :, :], ALU.mult))
                link(nc.vector.tensor_reduce(small[:, 3, :], sq_sb[:, :, :], AX_X, ALU.add))
                ins = nc.vector.tensor_scalar(small[:, 3, :], small[:, 3, :], 1e-24, None, ALU.max)
                rsqrt_by_pool(ins, done, out_sem, count)
                link(nc.vector.tensor_tensor(y_sb[:, :, :], z_sb[:, :, :], bc(small[:, 4, :]), ALU.mult))
                link(nc.vector.tensor_tensor(y_sb[:, :, :], y_sb[:, :, :], zone(xh, rows), ALU.add))
                norm_stats(done, out_sem, count + 1)
                return nc.vector.tensor_tensor(hn_sb[:, :, :], y_sb[:, :, :], bc(small[:, 7, :]), ALU.mult)

            def finish1(e):
                dve.wait_ge(s_z, e + 1)
                if not (isinstance(e, int) and e == 0):
                    dve.wait_ge(s_h, e)
                finish1_steps(e * BR, s_var, s_root, e * 2 + 1).then_inc(s_hn, 1)

            def body(q, e, par, g, gdyn, first=False):
                for k in range(BR):
                    r8 = par * BR + k
                    for c in range(NC):
                        check(e * BR + k, r8, c)
                        if first:
                            continue
                        if (k, c) == (0, 2):
                            mean1(e - 1, 1 - par)
                        if (k, c) == (2, 2):
                            finish1(e - 1)
                    pack(q, e * BR + k, r8, g, gdyn)

            def fold_ok(e8):
                dve.wait_ge(s_chk, (e8 + 1) * 8 * NC)
                link(nc.vector.tensor_tensor(ok_min[:, :], ok_min[:, :], ok[:, :], ALU.min))

            base = link.n
            link.at(base)
            for e8 in range(2):
                for par in range(2):
                    e = 2 * e8 + par
                    body(0, e, par, e8, None, first=(e == 0))
                fold_ok(e8)
            base += link.n
            for q in range(1, NQ):
                with dve.Fori(0, 2) as i8:
                    link.at(i8 * (2 * LINKS1 + 1) + base)
                    for par in range(2):
                        body(q, i8 * 2 + (q * QB + par), par, None, i8)
                    fold_ok(i8 + 2 * q)
                    assert link.n == 2 * LINKS1 + 1, link.n
                base += 2 * link.n
            link.at(base)

            def unpack(q, n, r8, g, gdyn):
                dve.wait_ge(s_sum, NB + n - 1)
                shift = (ALU.logical_shift_left, 6 - r8) if r8 < 7 else (ALU.logical_shift_right, 1)
                nc.vector.tensor_scalar(words(t_sb[:, r8 % 2, low(q):NB, :]), plane(q, g, gdyn),
                                        shift[1], BIT4, shift[0], ALU.bitwise_and).then_inc(s_unp, 1)

            def mean2(e):
                dve.wait_ge(s_low, e + NBATCH + 1)
                dve.wait_ge(s_catps, e + NBATCH)
                nc.vector.scalar_tensor_tensor(out=cat[:, :, F:2 * F], in0=part_sum[:, :, :], scalar=0.5,
                                               in1=bc(zdeg(e * BR)), op0=ALU.mult,
                                               op1=ALU.mult).then_inc(s_mean, 1)

            def finish2_steps(rows, dst, done, out_sem, count):
                link(nc.vector.tensor_tensor(y_sb[:, :, :], z_sb[:, :, :], zone(xh, rows), ALU.add))
                norm_stats(done, out_sem, count)
                return nc.vector.tensor_tensor(dst, y_sb[:, :, :], bc(small[:, 7, :]), ALU.mult)

            def finish2(e, par):
                dve.wait_ge(s_z, e + NBATCH + 1)
                if not (isinstance(e, int) and e < 2):
                    dve.wait_ge(s_out[par], (e - par) * 8)
                finish2_steps(e * BR, o_sb[:, par, :, :], s_var, s_root, e + (2 * NBATCH + 1)).then_inc(s_o, 1)

            dve.wait_ge(s_pack, NB)
            unpack(0, 0, 0, 0, None)
            mean1(NBATCH - 1, 1)
            link(nc.vector.tensor_reduce(ok_one[:, 0:1], ok_min[:, :], AX_X, ALU.min))
            nc.vector.tensor_scalar(ok_one[:, 1:2], ok_one[:, 0:1], float(CH), None, ALU.is_lt).then_inc(s_bad, 1)
            unpack(0, 1, 1, 0, None)
            finish1(NBATCH - 1)
            dve.wait_ge(s_badps, 1)
            nc.vector.tensor_copy(bad_i[0:1, 0:1], c_ps[0:1, 0, 0:1]).then_inc(s_flag, 1)

            def upper_body(q, e, par, g, gdyn, first=-1):
                for k in range(BR):
                    if not (first == 0 and k < 2):
                        unpack(q, e * BR + k, par * BR + k, g, gdyn)
                    if k == 1 and first not in (0, 1):
                        finish2(e - 2, par)
                    if k == 2 and first != 0:
                        mean2(e - 1)

            for e in range(QB):
                upper_body(0, e, e % 2, e // 2, None, first=e)
            base += link.n
            for q in range(1, NQ):
                with dve.Fori(0, 2) as i8:
                    link.at(i8 * (2 * LINKS2) + base)
                    for par in range(2):
                        upper_body(q, i8 * 2 + (q * QB + par), par, None, i8)
                    assert link.n == 2 * LINKS2, link.n
                base += 2 * link.n
            link.at(base)
            finish2(NBATCH - 2, 0)
            mean2(NBATCH - 1)
            finish2(NBATCH - 1, 1)
            base += link.n

            def general_dve():
                gb = base
                dve.sem_inc(g_took, 1)
                for layer in range(2):
                    dve.wait_ge(g_x, 16)
                    if layer:
                        dve.wait_ge(g_h, NBATCH)
                    nc.vector.memset(g_feat[:, :, F:F + 1], 1.0)
                    nc.vector.tensor_copy(g_feat[:, :, 0:F], xh[:, :, :]).then_inc(g_ready, 1)
                    with dve.Fori(0, NB) as n:
                        this = count(dve, (n + (layer * NB + 1)) * GQ + 1)
                        settle(dve)
                        dve.wait_ge(g_use, this)
                        nc.vector.tensor_copy(g_agg[:, bass.ds(n, 1), :].rearrange("p a f -> p (a f)"),
                                              s_ps[0][:, 0:F + 1]).then_inc(g_took, 1)
                    dve.wait_ge(g_took, (layer + 1) * NB + 1)
                    with dve.Fori(0, NBATCH) as e:
                        b = e + layer * NBATCH
                        per = LINKS1 + 1 if layer == 0 else LINKS2
                        link.at(e * per + gb)
                        total = g_agg[:, bass.ds(e * BR, BR), 0:F]
                        deg = g_agg[:, bass.ds(e * BR, BR), F:F + 1].rearrange("p k o -> p (k o)")
                        old = count(dve, b + 1)
                        settle(dve)
                        dve.wait_ge(g_catps, old)
                        nc.vector.tensor_copy(cat[:, :, 0:F], zone(xh, e * BR)).then_inc(g_cat, 1)
                        if layer == 0:
                            mean1_steps(total, deg, e * BR, 1.0).then_inc(g_cat, 1)
                        else:
                            nc.vector.tensor_tensor(cat[:, :, F:2 * F], total, bc(zdeg(e * BR)),
                                                    ALU.mult).then_inc(g_cat, 1)
                        dve.wait_ge(g_z, b + 1)
                        if layer == 0:
                            link(finish1_steps(e * BR, g_var, g_root, e * 2 + 1), settle)
                            nc.vector.tensor_copy(zone(xh, e * BR), hn_sb[:, :, :]).then_inc(g_h, 1)
                        else:
                            dve.wait_ge(g_out, e * 16 + 16)
                            finish2_steps(e * BR, o_sb[:, 0, :, :], g_var, g_root, e + (2 * NBATCH + 1)).then_inc(g_o, 1)
                        assert link.n == per, link.n
                    gb += NBATCH * per
            if_bad(dve, general_dve)

        @block.gpsimd
        def _(pool):
            link = Links(pool, s_pool)

            link(nc.gpsimd.memset(ones_f[:, :], 1.0))
            link(nc.gpsimd.memset(minus_half[:, :], -0.5))
            link(nc.gpsimd.memset(ident[:, :], 0.0))
            nc.gpsimd.affine_select(out=ident[:, :], in_=ident[:, :], compare_op=ALU.not_equal, fill=1.0,
                                         base=0, pattern=[[-1, P]], channel_multiplier=1).then_inc(s_const, 1)

            def split(dst, src, tmp, done):
                link(nc.gpsimd.tensor_copy(dst[0], src), settle)
                link(nc.gpsimd.tensor_tensor(tmp, src, dst[0], ALU.subtract), settle)
                link(nc.gpsimd.tensor_copy(dst[1], tmp), settle)
                nc.gpsimd.tensor_tensor(dst[2], tmp, dst[1], ALU.subtract).then_inc(done, 1)

            pool.wait_ge(s_x[3], 16)
            split([Z[:, 3 * CB:, PARTS + i * F:PARTS + (i + 1) * F] for i in range(3)],
                  xh[:, 3 * CB:, :], split_p, s_xp)

            def add_parts(dst, src, extra=None):
                link(nc.gpsimd.tensor_tensor(dst, src[:, :, 0:F], src[:, :, F:2 * F], ALU.add), settle)
                ins = nc.gpsimd.tensor_tensor(dst, dst, src[:, :, 2 * F:3 * F], ALU.add)
                if extra is not None:
                    link(ins, settle)
                    ins = nc.gpsimd.tensor_tensor(dst, dst, extra, ALU.add)
                return ins

            def root(i, wait, count, done):
                pool.wait_ge(wait, count)
                src, dst = ((3, 4), (6, 7))[i]
                nc.gpsimd.tensor_tensor(small[:, dst, :], small[:, src, :], minus_half[:, :],
                                        ALU.pow).then_inc(done, 1)

            def batch1(q, e, par):
                rows, old = count(pool, (e + 1) * BR), count(pool, e)
                settle(pool)
                pool.wait_ge(s_agg, rows)
                if not (isinstance(e, int) and e == 0):
                    pool.wait_ge(s_mean, old)
                if q:
                    link(add_parts(zone(lower, e * BR), agg[:, par, :, 0:PARTS]))
                add_parts(part_sum[:, :, :], agg[:, par, :, PARTS:2 * PARTS]).then_inc(s_low, 1)
                root(0, s_var, e * 2 + 1, s_root)
                root(1, s_var, e * 2 + 2, s_root)
                done = count(pool, e + 1)
                settle(pool)
                pool.wait_ge(s_hn, done)
                link(nc.gpsimd.tensor_copy(zone(xh, e * BR), hn_sb[:, :, :]), settle)
                split([Z[:, bass.ds(e * BR, BR), i * F:(i + 1) * F] for i in range(3)],
                      hn_sb[:, :, :], rest[:, :, :], s_h)

            def batch2(q, e, par):
                pool.wait_ge(s_agg, (e + 1) * BR + NB)
                pool.wait_ge(s_mean, e + NBATCH)
                add_parts(part_sum[:, :, :], agg[:, par, :, 0:PARTS],
                          zone(lower, e * BR) if q else None).then_inc(s_low, 1)

            for e in range(QB):
                batch1(0, e, e % 2)
            base = link.n
            for q in range(1, NQ):
                with pool.Fori(q * QB // 2, (q + 1) * QB // 2) as e2:
                    links = 7
                    link.at((e2 - q * QB // 2) * (2 * links) + base)
                    for par in range(2):
                        batch1(q, e2 * 2 + par, par)
                    assert link.n == 2 * links, link.n
                base += QB * links

            def root2(e):
                root(1, s_var, e + (2 * NBATCH + 1), s_root)

            link.at(base)
            batch2(0, 0, 0)
            for e in range(1, QB):
                if e > 1:
                    root2(e - 2)
                batch2(0, e, e % 2)
            base += link.n
            for q in range(1, NQ):
                with pool.Fori(0, QB // 2) as i2:
                    link.at(i2 * 4 + base)
                    for par in range(2):
                        e = i2 * 2 + (q * QB + par)
                        root2(e - 2)
                        batch2(q, e, par)
                    assert link.n == 4, link.n
                base += QB * 2
            root2(NBATCH - 2)
            root2(NBATCH - 1)

            def general_pool():
                with pool.Fori(0, NBATCH) as e:
                    root(0, g_var, e * 2 + 1, g_root)
                    root(1, g_var, e * 2 + 2, g_root)
                with pool.Fori(0, NBATCH) as e:
                    root(1, g_var, e + (2 * NBATCH + 1), g_root)
            if_bad(pool, general_pool)


def kernel(**inputs):
    import numpy as _np
    import concourse.bacc as _bacc
    from concourse import mybir as _mybir
    from concourse.bass_utils import run_bass_kernel_spmd as _run

    nc = _bacc.Bacc("TRN2", target_bir_lowering=False, num_devices=1)
    arrays, args = {}, []
    for name in ("x", "adj", "L0_gnn_W", "L0_gnn_b", "L1_gnn_W"):
        a = _np.ascontiguousarray(inputs[name])
        arrays[f"in_{name}"] = a
        args.append(nc.dram_tensor(f"in_{name}", a.shape, _mybir.dt.from_np(a.dtype), kind="ExternalInput").ap())
    res = nc.dram_tensor("out_h", (N, F), _mybir.dt.float32, kind="ExternalOutput").ap()
    gnn_kernel(nc, *args, res)
    r = _run(nc, [arrays], core_ids=[0])
    return r.results[0]["out_h"]
```

```python
from contextlib import ExitStack

import concourse.bass as bass
from concourse import mybir

F32 = mybir.dt.float32
BF16 = mybir.dt.bfloat16
F16 = mybir.dt.float16
FP8 = mybir.dt.float8e4
U8 = mybir.dt.uint8
U16 = mybir.dt.uint16
U32 = mybir.dt.uint32
I32 = mybir.dt.int32
ALU = mybir.AluOpType
ACT = mybir.ActivationFunctionType
AX_X = mybir.AxisListType.X

N = 8192
F = 64
P = 128
NB = N // P
CH = 2048
NC = N // CH
CB = CH // P
BR = 4
NBATCH = NB // BR
NQ = 4
QR = NB // NQ
QB = QR // BR
HP = 2 * F
XP = 3 * F
XW = XP + 1
SW = HP + XW
PK = P // 8
PKW = PK // 4
HS = CH // 1024
BIT4 = 0x40404040
EPS = 1e-5
H_SCALE = 2.0 ** 12
ROUND = 8388608.0


def low(q):
    return NB if q == NQ else max(0, QR * q - BR)


def width(s):
    return low(s + 1) - low(s)


def strip_base(s):
    return sum(QR * (t + 1) * width(t) * PKW for t in range(s))


class Links:

    def __init__(self, eng, sem, settle):
        self.eng, self.sem, self.settle, self.base, self.n = eng, sem, settle, 0, 0

    def __call__(self, ins):
        self.n += 1
        ins.then_inc(self.sem, 1)
        value = self.base + self.n
        if not isinstance(value, int):
            self.eng.compute_val(value)
            self.settle(self.eng)
        self.eng.wait_ge(self.sem, value)

    def at(self, base):
        self.base, self.n = base, 0


def gnn_kernel(nc, x, adj, w0, b0, w1, out):
    ctx = ExitStack()
    with ctx:
        def sb(name, shape, dt):
            return ctx.enter_context(nc.sbuf_tensor(name, shape, dt))

        def ps(name, shape, dt):
            return ctx.enter_context(nc.psum_tensor(name, shape, dt))

        def sem(name):
            return ctx.enter_context(nc.semaphore(name))

        a_in = sb("a_in", [P, NC, CH], F32)
        e8 = sb("e8", [P, NC, CH], FP8)
        pk = sb("pk", [P, 2, NB * PK], U8)
        t_sb = sb("t_sb", [P, NB, P], FP8)
        store = sb("store", [P, strip_base(NQ)], U32)
        u_sb = sb("u_sb", [P, (NQ - 1) * QR * P], FP8)
        x_all = sb("x_all", [P, HP + NB * (XW + 1)], BF16)
        h_parts = sb("h_parts", [P, NB, HP], F16)
        bias = sb("bias", [P, BR, F], F32)
        lower = sb("lower", [P, NB, F], F32)
        agg = sb("agg", [P, 2, BR, SW], F32)
        u_agg = sb("u_agg", [P, NQ - 1, HP], F32)
        half_sum = sb("half_sum", [P, NB, NC * HS], F32)
        junk = sb("junk", [P, 2, HS, 1024], U8)
        degp1 = sb("degp1", [P, NB], F32)
        rdeg2 = sb("rdeg2", [P, NB], F32)
        bad = sb("bad", [P, 2], F32)
        bad_i = sb("bad_i", [1, 1], I32)
        ident = sb("ident", [P, P], F32)
        pow_f = sb("pow_f", [P, PK], F32)
        pow_bf = sb("pow_bf", [P, PK], BF16)
        ones_f = sb("ones_f", [P, P], F32)
        w0_sb = sb("w0_sb", [P, F], F32)
        w1_raw = sb("w1_raw", [F, P], F32)
        w1_sb = sb("w1_sb", [P, F], F32)
        b0_sb = sb("b0_sb", [1, F], F32)
        part_sum = sb("part_sum", [P, BR, F], F32)
        nsum = sb("nsum", [P, BR, F], F32)
        cat = sb("cat", [P, BR, 2 * F], F32)
        cat_t = sb("cat_t", [P, BR, P], F32)
        z_sb = sb("z_sb", [P, BR, F], F32)
        y_sb = sb("y_sb", [P, BR, F], F32)
        sq_sb = sb("sq_sb", [P, BR, F], F32)
        hn_sb = sb("hn_sb", [P, BR, F], F32)
        o_sb = sb("o_sb", [P, 2, BR, F], F32)
        small = sb("small", [P, 8, BR], F32)
        minus_half = sb("minus_half", [P, BR], F32)
        x_parts = x_all[:, HP:].rearrange("p (b w) -> p b w", w=XW + 1)
        x_sb = lower
        split_v, split_p = (store[:, strip_base(NQ) - (i + 1) * CB * F:strip_base(NQ) - i * CB * F].bitcast(F32)
                            .rearrange("p (b f) -> p b f", f=F) for i in range(2))
        last_w = width(NQ - 1)
        v_sb = a_in[:, :, :].rearrange("p c i -> p (c i)").bitcast(FP8)[:, 0:2 * BR * last_w * P].rearrange(
            "p (s b i) -> p s b i", s=2, i=P)

        p_ps = [ps(f"p_ps{i}", [P, 512], F32) for i in range(2)]
        s_ps = [ps(f"s_ps{i}", [P, 512], F32) for i in range(2)]
        u_ps = [ps(f"u_ps{i}", [P, 512], F32) for i in range(2)]
        c_ps = ps("c_ps", [P, BR, P], F32)
        z_ps = ps("z_ps", [P, 512], F32)

        s_in = [sem(f"s_in{c}") for c in range(NC)]
        s_x = [sem(f"s_x{q}") for q in range(NQ)]
        s_w = sem("s_w")
        s_pow = sem("s_pow")
        s_w1t = sem("s_w1t")
        s_w1 = sem("s_w1")
        s_xv = sem("s_xv")
        s_xp = sem("s_xp")
        s_e = sem("s_e")
        s_half = sem("s_half")
        s_pps = sem("s_pps")
        s_pk = sem("s_pk")
        s_store = sem("s_store")
        s_t = sem("s_t")
        s_sum = sem("s_sum")
        s_agg = sem("s_agg")
        s_u = sem("s_u")
        s_ups = sem("s_ups")
        s_uagg = sem("s_uagg")
        s_uadd = sem("s_uadd")
        s_low = sem("s_low")
        s_feat = sem("s_feat")
        s_mean = sem("s_mean")
        s_catps = sem("s_catps")
        s_catt = sem("s_catt")
        s_zps = sem("s_zps")
        s_z = sem("s_z")
        s_var = sem("s_var")
        s_root = sem("s_root")
        s_hn = sem("s_hn")
        s_h = sem("s_h")
        s_v = sem("s_v")
        s_vps = sem("s_vps")
        s_vagg = sem("s_vagg")
        s_o = sem("s_o")
        s_out = [sem(f"s_out{i}") for i in range(2)]
        s_bad = sem("s_bad")
        s_badps = sem("s_badps")
        s_flag = sem("s_flag")
        s_dve = sem("s_dve")
        s_pool = sem("s_pool")

        out_v = out.rearrange("(e k p) f -> e p k f", k=BR, p=P)
        adj_v = adj.rearrange("(n p) c -> n p c", p=P)
        x_v = x.rearrange("(n p) f -> p n f", p=P)

        def words(ap):
            return ap.rearrange("p b i -> p (b i)").bitcast(U32).rearrange("p (b w) -> p b w", w=P // 4)

        pk_w = pk[:, :, :].rearrange("p s i -> p (s i)").bitcast(U32).rearrange("p (s w) -> p s w", s=2)

        def stored(s, row, rows):
            w = width(s) * PKW
            return store[:, bass.ds(row * w + strip_base(s), rows * w)]

        def e_in(e, first, last):
            return not isinstance(e, int) or first <= e <= last

        def in_steps(eng, step, link=None, links=0, first=0):
            body = range(4, NBATCH - 2, 2)
            for e in range(first, body.start):
                step(e, e % 2)
            base = link.base + link.n if link else 0
            if link:
                link.at(base)
            with eng.Fori(0, len(body)) as i2:
                if link:
                    link.at(i2 * (2 * links) + base)
                for par in range(2):
                    step(i2 * 2 + (body.start + par), par)
            if link:
                assert link.n == 2 * links, link.n
                link.at(base + len(body) * 2 * links)
            for e in range(body.start + 2 * len(body), NBATCH + 3):
                step(e, e % 2)

        def zone(t, b, n=BR):
            return t[:, bass.ds(b, n), :]

        def zdeg(rows):
            return rdeg2[:, bass.ds(rows, BR)]

        g_feat = store[:, 0:NB * (F + 1)].bitcast(F32).rearrange("p (n f) -> p n f", f=F + 1)
        g_agg = store[:, NB * (F + 1):2 * NB * (F + 1)].bitcast(F32).rearrange("p (n f) -> p n f", f=F + 1)
        g_t = store[:, 2 * NB * (F + 1):2 * NB * (F + 1) + 2 * BR * P].bitcast(F32).rearrange(
            "p (s b i) -> p s b i", s=2, i=P)
        GQ = NB // BR
        tf_ps = [t[:, :].rearrange("p (b i) -> p b i", i=P) for t in p_ps]
        g_x = sem("g_x")
        g_in = [sem(f"g_in{c}") for c in range(NC)]
        g_tps = sem("g_tps")
        g_tsb = sem("g_tsb")
        g_use = sem("g_use")
        g_took = sem("g_took")
        g_ready = sem("g_ready")
        g_cat = sem("g_cat")
        g_catps = sem("g_catps")
        g_catt = sem("g_catt")
        g_zps = sem("g_zps")
        g_z = sem("g_z")
        g_var = sem("g_var")
        g_root = sem("g_root")
        g_o = sem("g_o")
        g_out = sem("g_out")
        s_const = sem("s_const")

        def count(eng, value):
            if not isinstance(value, int):
                eng.compute_val(value)
            return value

        def settle(eng):
            eng.wait_ge(s_const, 1)

        def if_bad(eng, general):
            eng.wait_ge(s_flag, 1)
            verdict = eng.value_load(bad_i[0:1, 0:1], min_val=0, max_val=P)
            with eng.If(verdict != 0):
                for i in range(2):
                    eng.wait_ge(s_out[i], 16 * NBATCH // 2)
                general()

        block = ctx.enter_context(nc.Block())

        @block.sync
        def _(sp):
            def load_row(n, first=False):
                for c in range(NC):
                    if not first:
                        sp.wait_ge(s_e, (n - 1) * NC + c + 1)
                        sp.wait_ge(s_half, (n - 1) * NC + c + 1)
                    src = adj_v[0, :, c * CH:(c + 1) * CH] if first else \
                        adj_v[bass.ds(n, 1), :, c * CH:(c + 1) * CH].rearrange("a p c -> (a p) c")
                    sp.dma_start(a_in[:, c, :], src).then_inc(s_in[c], 16)

            load_row(0, first=True)
            with sp.Fori(1, NB) as n:
                load_row(n)

            with sp.Fori(0, NBATCH // 2) as e2:
                for i in range(2):
                    e = e2 * 2 + i
                    sp.wait_ge(s_o, e + 1)
                    sp.dma_start(out_v[bass.ds(e, 1), :, :, :].rearrange("a p k f -> (a p) k f"),
                                 o_sb[:, i, :, :]).then_inc(s_out[i], 16)
            for i in range(2):
                sp.wait_ge(s_out[i], 16 * NBATCH // 2)

            def general_sp():
                sp.sem_inc(g_out, 16)
                for q in range(NQ):
                    sp.dma_start(g_feat[:, q * CB:(q + 1) * CB, 0:F], x_v[:, q * CB:(q + 1) * CB, :]).then_inc(g_x, 16)
                for layer in range(2):
                    with sp.Fori(0, NB) as n:
                        for c in range(NC):
                            sp.wait_ge(g_tps, n * GQ + (layer * NB * GQ + 1))
                            sp.dma_start(a_in[:, c, :], adj_v[bass.ds(n, 1), :, c * CH:(c + 1) * CH]
                                         .rearrange("a p c -> (a p) c")).then_inc(g_in[c], 16)
                with sp.Fori(0, NBATCH) as e:
                    sp.wait_ge(g_o, e + 1)
                    sp.dma_start(out_v[bass.ds(e, 1), :, :, :].rearrange("a p k f -> (a p) k f"),
                                 o_sb[:, 0, :, :]).then_inc(g_out, 16)
                sp.wait_ge(g_out, 16 * NBATCH + 16)
            if_bad(sp, general_sp)

        @block.tensor
        def _(pe):
            def pack_chunk(n, c):
                this = count(pe, n * NC + c + 1)
                old = count(pe, (n - 1) * 2 + c // 2 + 1) if c % 2 == 0 and not (isinstance(n, int) and n == 0) else None
                settle(pe)
                pe.wait_ge(s_e, this)
                if old is not None:
                    pe.wait_ge(s_pk, old)
                for b in range(CB):
                    at = ((c % 2) * CB + b) * PK
                    last = nc.tensor.matmul(p_ps[c // 2][:, at:at + PK], e8[:, c, b * P:(b + 1) * P],
                                            pow_bf[:, :], start=True, stop=True)
                last.then_inc(s_pps, 1)

            def sum_quarter(q, n, k, i, first=False):
                if i % 2 == 0:
                    this = count(pe, n * 2 + (i // 2 + 1))
                    old = count(pe, n - 1) if i == 0 and not (isinstance(n, int) and n < 2) else None
                    settle(pe)
                    pe.wait_ge(s_t, this)
                    if old is not None:
                        pe.wait_ge(s_agg, old)
                if first:
                    pe.wait_ge((s_xv, s_xp)[i // 2], i % 2 + 1)
                for b in range(i * CB, (i + 1) * CB):
                    if b == 0:
                        nc.tensor.matmul(s_ps[k % 2][:, 0:SW], t_sb[:, b, :], x_all[:, 0:SW],
                                         start=True, stop=False)
                    if b < low(q):
                        nc.tensor.matmul(s_ps[k % 2][:, 0:HP], t_sb[:, b, :], h_parts[:, b, :],
                                         start=False, stop=False)
                    if b:
                        last = nc.tensor.matmul(s_ps[k % 2][:, HP:SW], t_sb[:, b, :], x_parts[:, b, 0:XW],
                                                start=False, stop=(b == NB - 1))
                if i % 2:
                    last.then_inc(s_sum, 1)

            def catch_up(q, n, k, part):
                if part == 0:
                    this = count(pe, n - (QR - 1))
                    settle(pe)
                    pe.wait_ge(s_u, this)
                    pe.wait_ge(s_uagg, this)
                w = width(q - 1)
                split = (q + 1) // 2
                for r in (range(split), range(split, q))[part]:
                    for b in range(w):
                        last = nc.tensor.matmul(u_ps[r // 2][:, (r % 2) * HP:(r % 2 + 1) * HP],
                                                u_sb[:, (r * w + b) * P:(r * w + b + 1) * P],
                                                h_parts[:, low(q - 1) + b, :], start=(b == 0), stop=(b == w - 1))
                    if r == q - 1:
                        last.then_inc(s_ups, 1)

            def transpose_cat(e):
                pe.wait_ge(s_feat, e + 1)
                pe.wait_ge(s_mean, e + 1)
                for k in range(BR):
                    last = nc.tensor.transpose(c_ps[:, k, :], cat[:, k, :], ident[:, :])
                last.then_inc(s_catps, 1)

            def dense_products(w, bias):
                for k in range(BR):
                    last = nc.tensor.matmul(z_ps[:, k * F:(k + 1) * F], cat_t[:, k, :], w[:, :],
                                            start=True, stop=not bias)
                    if bias:
                        last = nc.tensor.matmul(z_ps[:, k * F:(k + 1) * F], ones_f[0:1, :], b0_sb[0:1, :],
                                                start=False, stop=True)
                return last

            def dense(e, w, bias):
                pe.wait_ge(s_catt, e + 1)
                dense_products(w, bias).then_inc(s_zps, 1)

            def body(q, e, first=False):
                for k in range(BR):
                    n = e * BR + k
                    for c in range(NC):
                        pack_chunk(n, c)
                        if q and k == 0 and c == 0:
                            pe.wait_ge(s_h, QB * q - 1)
                        if not (first and k == 0):
                            sum_quarter(q, n - 1, (k - 1) % BR, c, first=first and k == 1)
                        if q and c < 2:
                            catch_up(q, n, k, c)
                        if not first and k == 2:
                            if c == 1:
                                transpose_cat(e - 1)
                            if c == 3:
                                dense(e - 1, w0_sb, False)

            def general_pe():
                for t in (g_tps, g_use, g_catps):
                    pe.sem_inc(t, 1)
                for layer in range(2):
                    w, bias = ((w0_sb, True), (w1_sb, False))[layer]

                    def transpose_group(n, g):
                        if g % (GQ // NC) == 0:
                            pe.wait_ge(g_in[g * NC // GQ], n * 16 + (layer * NB + 1) * 16)
                        if g >= 2:
                            pe.wait_ge(g_tsb, n * GQ + (layer * NB * GQ + g))
                        for b in range(BR):
                            col = (g * BR + b) * P
                            last = nc.tensor.transpose(tf_ps[g % 2][:, b, :],
                                                       a_in[:, col // CH, col % CH:col % CH + P], ident[:, :])
                        last.then_inc(g_tps, 1)

                    pe.wait_ge(g_ready, layer * NBATCH + 1)
                    with pe.Fori(0, NB) as n:
                        pe.wait_ge(g_tsb, n * GQ + (layer * NB * GQ + 1))
                        pe.wait_ge(g_took, n + (layer * NB + 1))
                        transpose_group(n, 0)
                        for g in range(GQ):
                            if g + 1 < GQ:
                                transpose_group(n, g + 1)
                            pe.wait_ge(g_tsb, n * GQ + (layer * NB * GQ + g + 2))
                            for b in range(BR):
                                last = nc.tensor.matmul(s_ps[0][:, 0:F + 1], g_t[:, g % 2, b, :],
                                                        g_feat[:, g * BR + b, :],
                                                        start=(g == 0 and b == 0), stop=(g == GQ - 1 and b == BR - 1))
                            last.then_inc(g_use, 1)
                    with pe.Fori(0, NBATCH) as e:
                        b = e + layer * NBATCH
                        pe.wait_ge(g_cat, b + 1)
                        for k in range(BR):
                            last = nc.tensor.transpose(c_ps[:, k, :], cat[:, k, :], ident[:, :])
                        last.then_inc(g_catps, 1)
                        pe.wait_ge(g_catt, b + 1)
                        dense_products(w, bias).then_inc(g_zps, 1)

            pe.sem_inc(s_ups, 1)
            pe.wait_ge(s_const, 1)
            pe.wait_ge(s_pow, 1)
            pe.wait_ge(s_w, 48)
            nc.tensor.transpose(c_ps[:, 0, 0:F], w1_raw[:, :], ident[0:F, 0:F]).then_inc(s_w1t, 1)
            for k in range(BR):
                last = nc.tensor.matmul(z_ps[:, k * F:(k + 1) * F], ones_f[0:1, :], b0_sb[0:1, :],
                                        start=True, stop=True)
            last.then_inc(s_w1t, 1)
            pe.wait_ge(s_w1, 2)
            body(0, 0, first=True)
            for q in range(NQ):
                with pe.Fori(1 if q == 0 else q * QB, (q + 1) * QB) as e:
                    body(q, e)
            for i in range(NC):
                sum_quarter(NQ - 1, NB - 1, BR - 1, i)

            def strip_sums(par, k, cols):
                bank = (u_ps, s_ps)[par][k // 2]
                for b in cols:
                    last = nc.tensor.matmul(bank[:, (k % 2) * HP:(k % 2 + 1) * HP],
                                            v_sb[:, par, k * last_w + b, :], h_parts[:, low(NQ - 1) + b, :],
                                            start=(b == 0), stop=(b == last_w - 1))
                return last

            def second(e, par):
                if e_in(e, 0, NBATCH - 1):
                    this = count(pe, e + 1)
                    old = count(pe, e * 2 - 2) if not (isinstance(e, int) and e < 2) else None
                    settle(pe)
                    pe.wait_ge(s_v, this)
                    if old is not None:
                        pe.wait_ge(s_vagg, old)
                for k in range(BR):
                    if e_in(e, 0, NBATCH - 1):
                        last = strip_sums(par, k, range(last_w))
                        if k % 2:
                            last.then_inc(s_vps, 1)
                    if k == 2 and e_in(e, 1, NBATCH):
                        transpose_cat(e + NBATCH - 1)
                if e_in(e, 1, NBATCH):
                    dense(e + NBATCH - 1, w1_sb, False)

            known = last_w - BR
            pe.wait_ge(s_uagg, (NQ - 1) * QR + 1)
            pe.wait_ge(s_v, 1)
            pe.wait_ge(s_h, NBATCH - 1)
            transpose_cat(NBATCH - 1)
            strip_sums(0, 0, range(known))
            dense(NBATCH - 1, w0_sb, False)
            strip_sums(0, 2, range(known))
            pe.wait_ge(s_bad, 1)
            nc.tensor.matmul(c_ps[0:1, 0, 0:1], bad[:, 1:2], ones_f[:, 0:1], start=True,
                             stop=True).then_inc(s_badps, 1)
            pe.wait_ge(s_h, NBATCH)
            for k in range(BR):
                last = strip_sums(0, k, range(known if k % 2 == 0 else 0, last_w))
                if k % 2:
                    last.then_inc(s_vps, 1)
            pe.wait_ge(s_agg, NB)
            in_steps(pe, second, first=1)
            if_bad(pe, general_pe)

        @block.scalar
        def _(act):
            for q in (0, 2, 1, 3):
                act.dma_start(x_sb[:, q * CB:(q + 1) * CB, :], x_v[:, q * CB:(q + 1) * CB, :]).then_inc(s_x[q], 16)
            act.dma_start(w0_sb[:, :], w0[:, :]).then_inc(s_w, 16)
            act.dma_start(w1_raw[:, :], w1[:, :]).then_inc(s_w, 16)
            act.dma_start(b0_sb[0:1, :], b0.unsqueeze(0)).then_inc(s_w, 16)
            act.sem_inc(s_uagg, 1)

            halves = [a_in[:, c, :].bitcast(U16).rearrange("p (b two) -> p b two", two=2)[:, :, 1]
                      for c in range(NC)]

            def sum_halves(n, c):
                this = count(act, n * 16 + 16)
                old = count(act, n * NC + c - 1) if not (isinstance(n, int) and n * NC + c < 2) else None
                settle(act)
                act.wait_ge(s_in[c], this)
                if old is not None:
                    act.wait_ge(s_half, old)
                for i in range(HS):
                    ins = nc.scalar.activation(
                        junk[:, c % 2, i, :], halves[c][:, i * 1024:(i + 1) * 1024], ACT.Copy, scale=1.0 / 128,
                        accum_out=half_sum[:, bass.ds(n, 1), c * HS + i:c * HS + i + 1].rearrange("p a b -> p (a b)"))
                    if i == HS - 1:
                        ins.then_inc(s_half, 1)

            def take_packed(n, slot, h):
                act.wait_ge(s_pps, n * NC + 2 * h + 2)
                if not (isinstance(n, int) and n < 2):
                    act.wait_ge(s_t, n * 2 + (h - 3))
                    act.wait_ge(s_store, n - 1)
                nc.scalar.copy(pk[:, slot, h * 512:(h + 1) * 512], p_ps[h][:, :]).then_inc(s_pk, 1)

            def take_sums(n, e, slot, k, free):
                act.wait_ge(s_sum, n * 2 + 2)
                if k == 0 and free:
                    act.wait_ge(s_low, e - 1)
                    act.wait_ge(s_mean, e - 1)
                nc.scalar.copy(agg[:, slot, k, :], s_ps[k % 2][:, 0:SW]).then_inc(s_agg, 1)

            def take_catch_up(q, n):
                act.wait_ge(s_ups, n - (QR - 2))
                act.wait_ge(s_uadd, n - (QR - 1))
                for r in range(0, q, 2):
                    rows = min(2, q - r)
                    ins = nc.scalar.copy(u_agg[:, r:r + rows, :].rearrange("p r f -> p (r f)"),
                                         u_ps[r // 2][:, 0:rows * HP])
                ins.then_inc(s_uagg, 1)

            def take_cat(e):
                act.wait_ge(s_catps, e + 1)
                if not (isinstance(e, int) and e == 0):
                    act.wait_ge(s_zps, e)
                nc.scalar.copy(cat_t[:, :, :].rearrange("p k i -> p (k i)"),
                               c_ps[:, :, :].rearrange("p k i -> p (k i)")).then_inc(s_catt, 1)

            def take_z(e, read, value):
                act.wait_ge(s_zps, e + (NBATCH + 1))
                act.wait_ge(read, value)
                nc.scalar.activation(z_sb[:, :, :].rearrange("p k i -> p (k i)"), z_ps[:, 0:BR * F],
                                     ACT.Copy, scale=1.0 / H_SCALE).then_inc(s_z, 1)

            def body(q, e, par, first=False):
                for k in range(BR):
                    n = e * BR + k
                    lead = first and k == 0
                    sum_halves(n, 0)
                    if not lead:
                        take_packed(n - 1, (k - 1) % 2, 0)
                    if not first and k == 3:
                        take_cat(e - 1)
                    sum_halves(n, 1)
                    sum_halves(n, 2)
                    if not lead:
                        take_packed(n - 1, (k - 1) % 2, 1)
                    if k > 1:
                        take_sums(n - 2, e, par, k - 2, not (isinstance(e, int) and e < 2))
                    elif not first:
                        take_sums(n - 2, e - 1, 1 - par, k + 2, False)
                    sum_halves(n, 3)
                    if q:
                        take_catch_up(q, n)

            def general_act():
                act.sem_inc(g_tsb, 1)
                for layer in range(2):
                    with act.Fori(0, NB) as n:
                        for g in range(GQ):
                            act.wait_ge(g_tps, n * GQ + (layer * NB * GQ + g + 2))
                            if g >= 2:
                                act.wait_ge(g_use, n * GQ + (layer * NB * GQ + g))
                            else:
                                act.wait_ge(g_use, n * GQ + (layer * NB * GQ + 1))
                            nc.scalar.copy(g_t[:, g % 2, :, :], tf_ps[g % 2]).then_inc(g_tsb, 1)
                    with act.Fori(0, NBATCH) as e:
                        b = e + layer * NBATCH
                        act.wait_ge(g_catps, b + 2)
                        nc.scalar.copy(cat_t[:, :, :], c_ps[:, :, :]).then_inc(g_catt, 1)
                        act.wait_ge(g_zps, b + 1)
                        nc.scalar.activation(z_sb[:, :, :].rearrange("p k i -> p (k i)"), z_ps[:, 0:BR * F],
                                             ACT.Copy if layer else ACT.Relu).then_inc(g_z, 1)

            act.wait_ge(s_w1t, 1)
            nc.scalar.copy(w1_sb[:, :], c_ps[:, 0, 0:F]).then_inc(s_w1, 1)
            act.wait_ge(s_w1t, 2)
            nc.scalar.copy(bias[:, :, :].rearrange("p k f -> p (k f)"), z_ps[:, 0:BR * F]).then_inc(s_w1, 1)
            for e in range(QB):
                body(0, e, e % 2, first=(e == 0))
            for q in range(1, NQ):
                with act.Fori(q * QB // 2, (q + 1) * QB // 2) as e2:
                    for par in range(2):
                        body(q, e2 * 2 + par, par)
            for h in range(2):
                take_packed(NB - 1, (NB - 1) % 2, h)
            for k in range(BR - 2, BR):
                take_sums(NB - BR + k, NBATCH - 1, (NBATCH - 1) % 2, k, False)
            take_cat(NBATCH - 1)

            def second(e, par):
                for i in range(2):
                    if e_in(e, 0, NBATCH - 1):
                        act.wait_ge(s_vps, e * 2 + i + 1)
                        if i == 0:
                            act.wait_ge(s_low, e + NBATCH - 1)
                            act.wait_ge(s_mean, e + NBATCH - 1)
                        nc.scalar.copy(agg[:, par, 2 * i:2 * i + 2, 0:HP],
                                       (u_ps, s_ps)[par][i][:, 0:2 * HP].rearrange("p (k f) -> p k f", k=2)
                                       ).then_inc(s_vagg, 1)
                    if e_in(e, 1, NBATCH):
                        if i == 0:
                            take_cat(e + NBATCH - 1)
                        elif isinstance(e, int) and e == 1:
                            take_z(e - 1, s_hn, NBATCH)
                        else:
                            take_z(e - 1, s_var, e + (2 * NBATCH - 1))

            in_steps(act, second)
            if_bad(act, general_act)

        MEAN1, FINISH1, FINISH2 = 5, 9, 5

        @block.vector
        def _(dve):
            link = Links(dve, s_dve, settle)
            bc = lambda t: t.unsqueeze(2).to_broadcast([P, BR, F])

            dve.wait_ge(s_const, 1)
            link(nc.vector.tensor_copy(pow_f[:, :], ident[:, P - PK:P]))
            for g in range(6, -1, -1):
                link(nc.vector.scalar_tensor_tensor(out=pow_f[:, :], in0=pow_f[:, :], scalar=2.0,
                                                    in1=ident[:, g * PK:(g + 1) * PK], op0=ALU.mult, op1=ALU.add))
            nc.vector.tensor_copy(pow_bf[:, :], pow_f[:, :]).then_inc(s_pow, 1)
            link(nc.vector.memset(x_parts[:, :, XP:XW], 1.0))
            link(nc.vector.memset(x_all[:, 0:HP], 0.0))

            def split_x(q):
                dve.wait_ge(s_x[q], 16)
                cols = slice(q * CB, (q + 1) * CB)
                hi, mid, lo = (x_parts[:, cols, i * F:(i + 1) * F] for i in range(3))
                link(nc.vector.tensor_copy(hi, x_sb[:, cols, :]))
                link(nc.vector.tensor_tensor(split_v, x_sb[:, cols, :], hi, ALU.subtract))
                link(nc.vector.tensor_copy(mid, split_v))
                nc.vector.tensor_tensor(lo, split_v, mid, ALU.subtract).then_inc(s_xv, 1)
                dve.wait_ge(s_xv, q + 1)

            def compare(n, c):
                t = n * NC + c
                this = count(dve, n * 16 + 16)
                old = count(dve, t - (NC - 1)) if not (isinstance(n, int) and n == 0) else None
                settle(dve)
                dve.wait_ge(s_in[c], this)
                if old is not None:
                    dve.wait_ge(s_pps, old)
                nc.vector.tensor_scalar(e8[:, c, :], a_in[:, c, :], 1.0, None, ALU.is_equal,
                                        saturate=False).then_inc(s_e, 1)

            def unpack_planes(dst, src):
                for g in range(8):
                    op, by = (ALU.logical_shift_left, 6 - g) if g < 7 else (ALU.logical_shift_right, 1)
                    ins = nc.vector.tensor_scalar(dst[:, :, g * PKW:(g + 1) * PKW], src, by, BIT4, op, ALU.bitwise_and)
                return ins

            def unpack(n, slot, h):
                packed = count(dve, n * 2 + (h + 1))
                old = count(dve, n * 2 + (h - 1)) if not (isinstance(n, int) and n == 0) else None
                settle(dve)
                dve.wait_ge(s_pk, packed)
                if old is not None:
                    dve.wait_ge(s_sum, old)
                half = slice(h * NB // 2, (h + 1) * NB // 2)
                unpack_planes(words(t_sb[:, half, :]),
                              pk_w[:, slot, :].rearrange("p (b w) -> p b w", w=PKW)[:, half, :]).then_inc(s_t, 1)

            def unpack_piece(q, n):
                w = width(q - 1)
                rows = count(dve, (n - (q * QR - 1)) * q)
                old = count(dve, n - (QR - 1))
                settle(dve)
                dve.wait_ge(s_store, rows)
                dve.wait_ge(s_ups, old)
                unpack_planes(words(u_sb[:, 0:q * w * P].rearrange("p (b i) -> p b i", i=P)),
                              stored(q - 1, (n - q * QR) * q, q).rearrange("p (b w) -> p b w", w=PKW)).then_inc(s_u, 1)

            def mean1_steps(total, deg, rows, scale):
                link(nc.vector.tensor_scalar(degp1[:, bass.ds(rows, BR)], deg, scale, 1.0, ALU.mult, ALU.add))
                link(nc.vector.reciprocal(zdeg(rows), degp1[:, bass.ds(rows, BR)]))
                link(nc.vector.tensor_scalar(small[:, 1, :], degp1[:, bass.ds(rows, BR)], 1.0, None, ALU.max))
                link(nc.vector.reciprocal(small[:, 2, :], small[:, 1, :]))
                link(nc.vector.scalar_tensor_tensor(out=nsum[:, :, :], in0=total, scalar=scale,
                                                    in1=cat[:, :, 0:F], op0=ALU.mult, op1=ALU.add))
                return nc.vector.tensor_tensor(cat[:, :, F:2 * F], nsum[:, :, :], bc(small[:, 2, :]), ALU.mult)

            def mean1(e, par):
                this = count(dve, e + 1)
                settle(dve)
                dve.wait_ge(s_feat, this)
                dve.wait_ge(s_low, this)
                deg = agg[:, par, :, SW - 1:SW].rearrange("p k o -> p (k o)")
                mean1_steps(part_sum[:, :, :], deg, e * BR, 0.5).then_inc(s_mean, 1)

            def norms(done):
                link(nc.vector.scalar_tensor_tensor(out=sq_sb[:, :, :], in0=z_sb[:, :, :], scalar=0.0,
                                                    in1=z_sb[:, :, :], op0=ALU.max, op1=ALU.mult))
                link(nc.vector.tensor_reduce(small[:, 3, :], sq_sb[:, :, :], AX_X, ALU.add))
                nc.vector.tensor_scalar(small[:, 3, :], small[:, 3, :], 1e-24, None, ALU.max).then_inc(done, 1)

            def variances(src, done, scale=1.0):
                link(nc.vector.tensor_reduce(small[:, 5, :], src, AX_X, ALU.add))
                link(nc.vector.tensor_scalar(small[:, 5, :], small[:, 5, :], 1.0 / F, None, ALU.mult))
                link(nc.vector.tensor_tensor(y_sb[:, :, :], src, bc(small[:, 5, :]), ALU.subtract))
                link(nc.vector.tensor_tensor(sq_sb[:, :, :], y_sb[:, :, :], y_sb[:, :, :], ALU.mult))
                link(nc.vector.tensor_reduce(small[:, 6, :], sq_sb[:, :, :], AX_X, ALU.add))
                nc.vector.tensor_scalar(small[:, 6, :], small[:, 6, :], scale ** -2 / F, scale ** -2 * EPS,
                                        ALU.mult, ALU.add).then_inc(done, 1)

            def residual(root, value, done, scale=1.0):
                dve.wait_ge(root, value)
                link(nc.vector.scalar_tensor_tensor(out=y_sb[:, :, :], in0=z_sb[:, :, :], scalar=0.0,
                                                    in1=bc(small[:, 4, :]), op0=ALU.max, op1=ALU.mult))
                link(nc.vector.tensor_tensor(y_sb[:, :, :], y_sb[:, :, :], cat[:, :, 0:F], ALU.add))
                variances(y_sb[:, :, :], done, scale)

            def finish1(e, part):
                if part == 0:
                    if isinstance(e, int) and e == 0:
                        dve.wait_ge(s_w1, 2)
                    this = count(dve, e + 1)
                    settle(dve)
                    dve.wait_ge(s_zps, this)
                    link(nc.vector.tensor_tensor(z_sb[:, :, :], z_ps[:, 0:BR * F].rearrange("p (k f) -> p k f", f=F),
                                                 bias[:, :, :], ALU.add))
                    norms(s_var)
                if part == 1:
                    residual(s_root, e * 2 + 1, s_var, H_SCALE)
                if part == 2:
                    dve.wait_ge(s_root, e * 2 + 2)
                    if not (isinstance(e, int) and e == 0):
                        dve.wait_ge(s_h, e)
                    nc.vector.tensor_tensor(hn_sb[:, :, :], y_sb[:, :, :], bc(small[:, 7, :]),
                                            ALU.mult).then_inc(s_hn, 1)

            def body(q, e, par, first=False):
                late = not (isinstance(e, int) and e < 2)
                for k in range(BR):
                    n = e * BR + k
                    compare(n, 0)
                    if q:
                        unpack_piece(q, n)
                    if first and k == 0:
                        split_x(0)
                    compare(n, 1)
                    if first and k == 0:
                        split_x(1)
                    else:
                        unpack(n - 1, (k - 1) % 2, 0)
                    if late and k == 0:
                        finish1(e - 2, 1)
                    compare(n, 2)
                    if not first and k == 2:
                        mean1(e - 1, 1 - par)
                    compare(n, 3)
                    if not (first and k == 0):
                        unpack(n - 1, (k - 1) % 2, 1)
                    if late and k == 0:
                        finish1(e - 2, 2)
                    if not first and k == 3:
                        finish1(e - 1, 0)

            body(0, 0, 0, first=True)
            for e in range(1, QB):
                body(0, e, e % 2)
            base = link.n
            for q in range(1, NQ):
                with dve.Fori(0, QB // 2) as i2:
                    link.at(i2 * (2 * (MEAN1 + 1 + FINISH1)) + base)
                    for par in range(2):
                        body(q, i2 * 2 + (q * QB + par), par)
                    assert link.n == 2 * (MEAN1 + 1 + FINISH1), link.n
                base += QB // 2 * link.n
            link.at(base)

            def unpack_last(e, par):
                if isinstance(e, int) and e == 0:
                    dve.wait_ge(s_half, NB * NC)
                    dve.wait_ge(s_e, NB * NC)
                    dve.wait_ge(s_store, NB)
                if not (isinstance(e, int) and e < 2):
                    old = count(dve, e * 2 - 2)
                    settle(dve)
                    dve.wait_ge(s_vps, old)
                unpack_planes(words(v_sb[:, par, :, :]),
                              stored(NQ - 1, e * BR, BR).rearrange("p (b w) -> p b w", w=PKW)).then_inc(s_v, 1)

            def mean2(e):
                this, old = count(dve, e + NBATCH + 1), count(dve, e + NBATCH)
                settle(dve)
                dve.wait_ge(s_low, this)
                dve.wait_ge(s_catps, old)
                nc.vector.scalar_tensor_tensor(out=cat[:, :, F:2 * F], in0=part_sum[:, :, :], scalar=0.5,
                                               in1=bc(zdeg(e * BR)), op0=ALU.mult,
                                               op1=ALU.mult).then_inc(s_mean, 1)

            def finish2_steps(dst, done, root, value):
                variances(z_sb[:, :, :], done)
                dve.wait_ge(root, value)
                return nc.vector.tensor_tensor(dst, y_sb[:, :, :], bc(small[:, 7, :]), ALU.mult)

            def finish2(e, par):
                this = count(dve, e + (2 * NBATCH + 1))
                old = count(dve, (e - par) * 8) if not (isinstance(e, int) and e < 2) else None
                settle(dve)
                dve.wait_ge(s_root, this)
                if old is not None:
                    dve.wait_ge(s_out[par], old)
                nc.vector.tensor_tensor(o_sb[:, par, :, :], y_sb[:, :, :], bc(small[:, 7, :]),
                                        ALU.mult).then_inc(s_o, 1)

            unpack(NB - 1, (NB - 1) % 2, 0)
            finish1(NBATCH - 2, 1)
            unpack(NB - 1, (NB - 1) % 2, 1)
            finish1(NBATCH - 2, 2)
            unpack_last(0, 0)
            mean1(NBATCH - 1, 1)
            hs = half_sum[:, :, :].rearrange("p n j -> p (n j)")
            r_hs = t_sb[:, 0:CB, :].rearrange("p b i -> p (b i)").bitcast(F32)[:, 0:NB * NC * HS]
            rows = t_sb[:, CB:2 * CB, :].rearrange("p b i -> p (b i)").bitcast(F32)
            dve.wait_ge(s_sum, 2 * NB)
            link(nc.vector.tensor_scalar(r_hs, hs, ROUND, None, ALU.add))
            link(nc.vector.tensor_scalar(r_hs, r_hs, ROUND, None, ALU.subtract))
            link(nc.vector.tensor_tensor(r_hs, r_hs, hs, ALU.not_equal))
            link(nc.vector.tensor_reduce(bad[:, 0:1], r_hs, AX_X, ALU.max))
            link(nc.vector.tensor_reduce(rows[:, 0:NB], half_sum[:, :, :], AX_X, ALU.add))
            link(nc.vector.tensor_scalar(rows[:, NB:2 * NB], degp1[:, :], -1.0, 127.0, ALU.add, ALU.mult))
            link(nc.vector.tensor_tensor(rows[:, 0:NB], rows[:, 0:NB], rows[:, NB:2 * NB], ALU.not_equal))
            link(nc.vector.tensor_reduce(bad[:, 1:2], rows[:, 0:NB], AX_X, ALU.max))
            nc.vector.tensor_tensor(bad[:, 1:2], bad[:, 1:2], bad[:, 0:1], ALU.max).then_inc(s_bad, 1)
            for part in range(3):
                finish1(NBATCH - 1, part)
            dve.wait_ge(s_badps, 1)
            nc.vector.tensor_copy(bad_i[0:1, 0:1], c_ps[0:1, 0, 0:1]).then_inc(s_flag, 1)
            base += link.n
            link.at(base)

            def second(e, par):
                if e_in(e, 3, NBATCH + 2):
                    finish2(e - 3, 1 - par)
                if e_in(e, 2, NBATCH + 1):
                    dve.wait_ge(s_z, e - 1)
                    if e_in(e, 3, NBATCH + 1):
                        dve.wait_ge(s_o, e - 2)
                    variances(z_sb[:, :, :], s_var)
                if e_in(e, 1, NBATCH):
                    mean2(e - 1)
                if e_in(e, 0, NBATCH - 2):
                    unpack_last(e + 1, 1 - par)

            in_steps(dve, second, link, 5)
            base = link.base + link.n

            def general_dve():
                gb = base
                dve.sem_inc(g_took, 1)
                dve.wait_ge(g_x, 16 * NQ)
                nc.vector.memset(g_feat[:, :, F:F + 1], 1.0).then_inc(g_ready, 1)
                for layer in range(2):
                    with dve.Fori(0, NB) as n:
                        this = count(dve, (n + (layer * NB + 1)) * GQ + 1)
                        settle(dve)
                        dve.wait_ge(g_use, this)
                        nc.vector.tensor_copy(g_agg[:, bass.ds(n, 1), :].rearrange("p a f -> p (a f)"),
                                              s_ps[0][:, 0:F + 1]).then_inc(g_took, 1)
                    dve.wait_ge(g_took, (layer + 1) * NB + 1)
                    with dve.Fori(0, NBATCH) as e:
                        b = e + layer * NBATCH
                        per = MEAN1 + FINISH1 if layer == 0 else FINISH2
                        link.at(e * (per + 1) + gb)
                        total = g_agg[:, bass.ds(e * BR, BR), 0:F]
                        deg = g_agg[:, bass.ds(e * BR, BR), F:F + 1].rearrange("p k o -> p (k o)")
                        feat = g_feat[:, bass.ds(e * BR, BR), 0:F]
                        old = count(dve, b + 1)
                        settle(dve)
                        dve.wait_ge(g_catps, old)
                        link(nc.vector.tensor_copy(cat[:, :, 0:F], feat))
                        if layer == 0:
                            mean1_steps(total, deg, e * BR, 1.0).then_inc(g_cat, 1)
                        else:
                            nc.vector.tensor_tensor(cat[:, :, F:2 * F], total, bc(zdeg(e * BR)),
                                                    ALU.mult).then_inc(g_cat, 1)
                        dve.wait_ge(g_z, b + 1)
                        if layer == 0:
                            norms(g_var)
                            residual(g_root, e * 2 + 1, g_var)
                            this = count(dve, e * 2 + 2)
                            settle(dve)
                            dve.wait_ge(g_root, this)
                            nc.vector.tensor_tensor(feat, y_sb[:, :, :], bc(small[:, 7, :]),
                                                    ALU.mult).then_inc(g_ready, 1)
                        else:
                            dve.wait_ge(g_out, e * 16 + 16)
                            finish2_steps(o_sb[:, 0, :, :], g_var, g_root, e + (2 * NBATCH + 1)).then_inc(g_o, 1)
                        assert link.n == per + 1, link.n
                    gb += NBATCH * (per + 1)
            if_bad(dve, general_dve)

        FEATURES, SUMS, SPLIT, PIECE = 1, 2, 1, 1

        @block.gpsimd
        def _(pool):
            link = Links(pool, s_pool, settle)

            link(nc.gpsimd.memset(ones_f[:, :], 1.0))
            link(nc.gpsimd.memset(minus_half[:, :], -0.5))
            link(nc.gpsimd.memset(ident[:, :], 0.0))
            nc.gpsimd.affine_select(out=ident[:, :], in_=ident[:, :], compare_op=ALU.not_equal, fill=1.0,
                                    base=0, pattern=[[-1, P]], channel_multiplier=1).then_inc(s_const, 1)
            for q in range(1, NQ):
                w = width(q - 1) * PKW
                at = strip_base(q - 1) + (QR * q - 1) * w
                link(nc.gpsimd.memset(store[:, at:at + w], 0))

            def split_x(dst, src, tmp, done):
                link(nc.gpsimd.tensor_copy(dst[0], src))
                link(nc.gpsimd.tensor_tensor(tmp, src, dst[0], ALU.subtract))
                link(nc.gpsimd.tensor_copy(dst[1], tmp))
                nc.gpsimd.tensor_tensor(dst[2], tmp, dst[1], ALU.subtract).then_inc(done, 1)

            for q in (2, 3):
                pool.wait_ge(s_x[q], 16)
                if q == 3:
                    pool.wait_ge(s_xp, 1)
                cols = slice(q * CB, (q + 1) * CB)
                split_x([x_parts[:, cols, i * F:(i + 1) * F] for i in range(3)],
                        x_sb[:, cols, :], split_p, s_xp)
            pool.sem_inc(s_uadd, 1)
            pool.wait_ge(s_w1, 1)
            pool.wait_ge(s_xp, 2)
            link(nc.gpsimd.tensor_tensor(w1_sb[0:F, :], w1_sb[0:F, :], ident[0:F, 0:F], ALU.add))

            def add_parts(dst, src, extra=None):
                ins = nc.gpsimd.tensor_tensor(dst, src[:, :, 0:F], src[:, :, F:2 * F], ALU.add)
                rest = [src[:, :, i * F:(i + 1) * F] for i in range(2, src.shape[2] // F)]
                for t in rest + ([extra] if extra is not None else []):
                    link(ins)
                    ins = nc.gpsimd.tensor_tensor(dst, dst, t, ALU.add)
                return ins

            def root(i, wait, value, done):
                pool.wait_ge(wait, value)
                src, dst = ((3, 4), (6, 7))[i]
                nc.gpsimd.tensor_tensor(small[:, dst, :], small[:, src, :], minus_half[:, :],
                                        ALU.pow).then_inc(done, 1)

            def keep(q, n, slot):
                this = count(pool, n * 2 + 2)
                settle(pool)
                pool.wait_ge(s_pk, this)
                for s in range(q, NQ):
                    ins = nc.gpsimd.tensor_copy(stored(s, n, 1), pk_w[:, slot, low(s) * PKW:low(s + 1) * PKW])
                ins.then_inc(s_store, 1)

            def add_piece(q, n):
                this = count(pool, n - (QR - 2))
                settle(pool)
                pool.wait_ge(s_uagg, this)
                rows = zone(lower, (n - q * QR) * q, q)
                link(nc.gpsimd.tensor_tensor(u_agg[:, 0:q, 0:F], u_agg[:, 0:q, 0:F], u_agg[:, 0:q, F:2 * F], ALU.add))
                nc.gpsimd.tensor_tensor(rows, rows, u_agg[:, 0:q, 0:F], ALU.add).then_inc(s_uadd, 1)

            def features(e, old_e, parts):
                if not (isinstance(old_e, int) and old_e == 0):
                    old = count(pool, old_e)
                    settle(pool)
                    pool.wait_ge(s_catps, old)
                    if parts is x_parts:
                        pool.wait_ge(s_hn, old)
                width_p = XP if parts is x_parts else HP
                add_parts(cat[:, :, 0:F], parts[:, bass.ds(e * BR, BR), 0:width_p]).then_inc(s_feat, 1)

            def batch_sums(e, par):
                rows = count(pool, (e + 1) * BR)
                old = count(pool, e) if not (isinstance(e, int) and e == 0) else None
                settle(pool)
                pool.wait_ge(s_agg, rows)
                if old is not None:
                    pool.wait_ge(s_mean, old)
                link(add_parts(zone(lower, e * BR), agg[:, par, :, 0:HP]))
                add_parts(part_sum[:, :, :], agg[:, par, :, HP:HP + XP]).then_inc(s_low, 1)

            def split_h(e):
                this = count(pool, e + 1)
                settle(pool)
                pool.wait_ge(s_hn, this)
                hi, lo = (h_parts[:, bass.ds(e * BR, BR), i * F:(i + 1) * F] for i in range(2))
                link(nc.gpsimd.tensor_copy(hi, hn_sb[:, :, :]))
                nc.gpsimd.tensor_tensor(lo, hn_sb[:, :, :], hi, ALU.subtract).then_inc(s_h, 1)

            def finish(e):
                root(0, s_var, e * 2 + 1, s_root)
                root(1, s_var, e * 2 + 2, s_root)

            def body(q, e, par, first=False):
                late = not (isinstance(e, int) and e < 2)
                for k in range(BR):
                    n = e * BR + k
                    if late and k == 0:
                        finish(e - 2)
                    if not first and k == 1:
                        features(e - 1, e - 1, x_parts)
                        batch_sums(e - 1, 1 - par)
                    if not (first and k == 0):
                        keep(q, n - 1, (k - 1) % 2)
                    if late and k == 0:
                        split_h(e - 2)
                    if q:
                        add_piece(q, n)

            for e in range(QB):
                body(0, e, e % 2, first=(e == 0))
            base = link.n
            for q in range(1, NQ):
                with pool.Fori(0, QB // 2) as i2:
                    links = 2 * (FEATURES + SUMS + SPLIT + BR * PIECE)
                    link.at(i2 * links + base)
                    for par in range(2):
                        body(q, i2 * 2 + (q * QB + par), par)
                    assert link.n == links, link.n
                base += QB // 2 * links
            link.at(base)
            e = NBATCH - 1
            finish(e - 1)
            keep(NQ - 1, NB - 1, (NB - 1) % 2)
            split_h(e - 1)
            features(e, e, x_parts)
            batch_sums(e, e % 2)
            finish(e)
            split_h(e)
            pool.wait_ge(s_h, NBATCH)

            def second_features(e):
                features(e, e + NBATCH, h_parts)

            def second_sums(e, par):
                rows, old = count(pool, e * 2 + 2), count(pool, e + NBATCH)
                settle(pool)
                pool.wait_ge(s_vagg, rows)
                pool.wait_ge(s_mean, old)
                add_parts(part_sum[:, :, :], agg[:, par, :, 0:HP], zone(lower, e * BR)).then_inc(s_low, 1)

            def second_root(e):
                root(1, s_var, e + (2 * NBATCH + 1), s_root)

            def second(e, par):
                if e_in(e, 1, NBATCH):
                    second_sums(e - 1, 1 - par)
                if e_in(e, 2, NBATCH + 1):
                    second_root(e - 2)
                if e_in(e, 0, NBATCH - 1):
                    second_features(e)

            base += link.n
            link.at(base)
            in_steps(pool, second, link, 1)

            def general_pool():
                with pool.Fori(0, NBATCH) as e:
                    root(0, g_var, e * 2 + 1, g_root)
                    root(1, g_var, e * 2 + 2, g_root)
                with pool.Fori(0, NBATCH) as e:
                    root(1, g_var, e + (2 * NBATCH + 1), g_root)
            if_bad(pool, general_pool)


def kernel(**inputs):
    import numpy as _np
    import concourse.bacc as _bacc
    from concourse import mybir as _mybir
    from concourse.bass_utils import run_bass_kernel_spmd as _run

    nc = _bacc.Bacc("TRN2", target_bir_lowering=False, num_devices=1)
    arrays, args = {}, []
    for name in ("x", "adj", "L0_gnn_W", "L0_gnn_b", "L1_gnn_W"):
        a = _np.ascontiguousarray(inputs[name])
        arrays[f"in_{name}"] = a
        args.append(nc.dram_tensor(f"in_{name}", a.shape, _mybir.dt.from_np(a.dtype), kind="ExternalInput").ap())
    res = nc.dram_tensor("out_h", (N, F), _mybir.dt.float32, kind="ExternalOutput").ap()
    gnn_kernel(nc, *args, res)
    r = _run(nc, [arrays], core_ids=[0])
    return r.results[0]["out_h"]
```

```python
from contextlib import ExitStack

import concourse.bass as bass
from concourse import mybir

F32 = mybir.dt.float32
BF16 = mybir.dt.bfloat16
F16 = mybir.dt.float16
FP8 = mybir.dt.float8e4
U8 = mybir.dt.uint8
U16 = mybir.dt.uint16
U32 = mybir.dt.uint32
I32 = mybir.dt.int32
ALU = mybir.AluOpType
ACT = mybir.ActivationFunctionType
AX_X = mybir.AxisListType.X

N = 8192
F = 64
P = 128
NB = N // P
CH = 2048
NC = N // CH
CB = CH // P
BR = 4
NBATCH = NB // BR
START = [0] + list(range(NB // 4, NB + 1, NB // 8))
NQ = len(START) - 1
HP = 2 * F
XP = 3 * F
XW = XP + 1
SW = HP + XW
PK = P // 8
PKW = PK // 4
HS = CH // 1024
BIT4 = 0x40404040
EPS = 1e-5
H_SCALE = 2.0 ** 12
ROUND = 8388608.0


def low(q):
    return NB if q == NQ else max(0, START[q] - BR)


def width(s):
    return low(s + 1) - low(s)


def strip_base(s):
    return sum(START[t + 1] * width(t) * PKW for t in range(s))


def piece(q):
    return START[q] // (START[q + 1] - START[q])


def batches(q):
    return START[q] // BR, (START[q + 1] - START[q]) // BR


class Links:

    def __init__(self, eng, sem, settle):
        self.eng, self.sem, self.settle, self.base, self.n = eng, sem, settle, 0, 0

    def __call__(self, ins):
        self.n += 1
        ins.then_inc(self.sem, 1)
        value = self.base + self.n
        if not isinstance(value, int):
            self.eng.compute_val(value)
            self.settle(self.eng)
        self.eng.wait_ge(self.sem, value)

    def at(self, base):
        self.base, self.n = base, 0


def gnn_kernel(nc, x, adj, w0, b0, w1, out):
    ctx = ExitStack()
    with ctx:
        def sb(name, shape, dt):
            return ctx.enter_context(nc.sbuf_tensor(name, shape, dt))

        def ps(name, shape, dt):
            return ctx.enter_context(nc.psum_tensor(name, shape, dt))

        def sem(name):
            return ctx.enter_context(nc.semaphore(name))

        a_in = sb("a_in", [P, NC, CH], F32)
        e8 = sb("e8", [P, NC, CH], FP8)
        pk = sb("pk", [P, 2, NB * PK], U8)
        t_sb = sb("t_sb", [P, NB, P], FP8)
        store = sb("store", [P, strip_base(NQ)], U32)
        u_sb = sb("u_sb", [P, max(piece(q) * width(q - 1) for q in range(1, NQ)) * P], FP8)
        x_all = sb("x_all", [P, HP + NB * (XW + 1)], BF16)
        h_parts = sb("h_parts", [P, NB, HP], F16)
        bias = sb("bias", [P, BR, F], F32)
        lower = sb("lower", [P, NB, F], F32)
        agg = sb("agg", [P, 2, BR, SW], F32)
        u_agg = sb("u_agg", [P, max(map(piece, range(NQ))), HP], F32)
        half_sum = sb("half_sum", [P, NB, NC * HS], F32)
        junk = sb("junk", [P, 2, HS, 1024], U8)
        degp1 = sb("degp1", [P, NB], F32)
        rdeg2 = sb("rdeg2", [P, NB], F32)
        bad = sb("bad", [P, 2], F32)
        bad_i = sb("bad_i", [1, 1], I32)
        ident = sb("ident", [P, P], F32)
        pow_f = sb("pow_f", [P, PK], F32)
        pow_bf = sb("pow_bf", [P, PK], BF16)
        ones_f = sb("ones_f", [P, P], F32)
        w0_sb = sb("w0_sb", [P, F], F32)
        w1_raw = sb("w1_raw", [F, P], F32)
        w1_sb = sb("w1_sb", [P, F], F32)
        b0_sb = sb("b0_sb", [1, F], F32)
        part_sum = sb("part_sum", [P, BR, F], F32)
        nsum = sb("nsum", [P, BR, F], F32)
        cat = sb("cat", [P, BR, 2 * F], F32)
        cat_t = sb("cat_t", [P, BR, P], F32)
        z_sb = sb("z_sb", [P, BR, F], F32)
        y_sb = sb("y_sb", [P, BR, F], F32)
        sq_sb = sb("sq_sb", [P, BR, F], F32)
        hn_sb = sb("hn_sb", [P, BR, F], F32)
        o_sb = sb("o_sb", [P, 2, BR, F], F32)
        small = sb("small", [P, 8, BR], F32)
        minus_half = sb("minus_half", [P, BR], F32)
        x_parts = x_all[:, HP:].rearrange("p (b w) -> p b w", w=XW + 1)
        x_sb = lower
        split_v, split_p = (store[:, strip_base(NQ) - (i + 1) * CB * F:strip_base(NQ) - i * CB * F].bitcast(F32)
                            .rearrange("p (b f) -> p b f", f=F) for i in range(2))
        y2 = [y_sb[:, :, :], z_sb[:, :, :]]
        last_w = width(NQ - 1)
        v_sb = a_in[:, :, :].rearrange("p c i -> p (c i)").bitcast(FP8)[:, 0:2 * BR * last_w * P].rearrange(
            "p (s b i) -> p s b i", s=2, i=P)

        p_ps = [ps(f"p_ps{i}", [P, 512], F32) for i in range(2)]
        s_ps = [ps(f"s_ps{i}", [P, 512], F32) for i in range(2)]
        u_ps = [ps(f"u_ps{i}", [P, 512], F32) for i in range(2)]
        c_ps = ps("c_ps", [P, BR, P], F32)
        z_ps = ps("z_ps", [P, 512], F32)

        s_in = [sem(f"s_in{c}") for c in range(NC)]
        s_x = [sem(f"s_x{q}") for q in range(NC)]
        s_w = sem("s_w")
        s_pow = sem("s_pow")
        s_w1t = sem("s_w1t")
        s_w1 = sem("s_w1")
        s_xv = sem("s_xv")
        s_xp = sem("s_xp")
        s_e = sem("s_e")
        s_half = sem("s_half")
        s_pps = sem("s_pps")
        s_pk = sem("s_pk")
        s_store = sem("s_store")
        s_t = sem("s_t")
        s_sum = sem("s_sum")
        s_agg = sem("s_agg")
        s_u = sem("s_u")
        s_ups = sem("s_ups")
        s_uagg = sem("s_uagg")
        s_uadd = sem("s_uadd")
        s_part = sem("s_part")
        s_low = sem("s_low")
        s_feat = sem("s_feat")
        s_mean = sem("s_mean")
        s_catps = sem("s_catps")
        s_catt = sem("s_catt")
        s_zps = sem("s_zps")
        s_z = sem("s_z")
        s_var = sem("s_var")
        s_root = sem("s_root")
        s_hn = sem("s_hn")
        s_h = sem("s_h")
        s_v = sem("s_v")
        s_vps = sem("s_vps")
        s_vagg = sem("s_vagg")
        s_o = sem("s_o")
        s_out = [sem(f"s_out{i}") for i in range(2)]
        s_bad = sem("s_bad")
        s_badps = sem("s_badps")
        s_flag = sem("s_flag")
        s_dve = sem("s_dve")
        s_pool = sem("s_pool")

        out_v = out.rearrange("(e k p) f -> e p k f", k=BR, p=P)
        adj_v = adj.rearrange("(n p) c -> n p c", p=P)
        x_v = x.rearrange("(n p) f -> p n f", p=P)

        def words(ap):
            return ap.rearrange("p b i -> p (b i)").bitcast(U32).rearrange("p (b w) -> p b w", w=P // 4)

        pk_w = pk[:, :, :].rearrange("p s i -> p (s i)").bitcast(U32).rearrange("p (s w) -> p s w", s=2)

        def stored(s, row, rows):
            w = width(s) * PKW
            return store[:, bass.ds(row * w + strip_base(s), rows * w)]

        def e_in(e, first, last):
            return not isinstance(e, int) or first <= e <= last

        def in_steps(eng, step, link=None, links=0, first=0):
            body = range(6, NBATCH - 2, 2)
            for e in range(first, body.start):
                step(e, e % 2)
            base = link.base + link.n if link else 0
            if link:
                link.at(base)
            with eng.Fori(0, len(body)) as i2:
                if link:
                    link.at(i2 * (2 * links) + base)
                for par in range(2):
                    step(i2 * 2 + (body.start + par), par)
            if link:
                assert link.n == 2 * links, link.n
                link.at(base + len(body) * 2 * links)
            for e in range(body.start + 2 * len(body), NBATCH + 3):
                step(e, e % 2)

        def zone(t, b, n=BR):
            return t[:, bass.ds(b, n), :]

        def zdeg(rows):
            return rdeg2[:, bass.ds(rows, BR)]

        g_feat = store[:, 0:NB * (F + 1)].bitcast(F32).rearrange("p (n f) -> p n f", f=F + 1)
        g_agg = store[:, NB * (F + 1):2 * NB * (F + 1)].bitcast(F32).rearrange("p (n f) -> p n f", f=F + 1)
        g_t = store[:, 2 * NB * (F + 1):2 * NB * (F + 1) + 2 * BR * P].bitcast(F32).rearrange(
            "p (s b i) -> p s b i", s=2, i=P)
        GQ = NB // BR
        tf_ps = [t[:, :].rearrange("p (b i) -> p b i", i=P) for t in p_ps]
        g_x = sem("g_x")
        g_in = [sem(f"g_in{c}") for c in range(NC)]
        g_tps = sem("g_tps")
        g_tsb = sem("g_tsb")
        g_use = sem("g_use")
        g_took = sem("g_took")
        g_ready = sem("g_ready")
        g_cat = sem("g_cat")
        g_catps = sem("g_catps")
        g_catt = sem("g_catt")
        g_zps = sem("g_zps")
        g_z = sem("g_z")
        g_var = sem("g_var")
        g_root = sem("g_root")
        g_o = sem("g_o")
        g_out = sem("g_out")
        s_const = sem("s_const")

        def count(eng, value):
            if not isinstance(value, int):
                eng.compute_val(value)
            return value

        def settle(eng):
            eng.wait_ge(s_const, 1)

        def if_bad(eng, general):
            eng.wait_ge(s_flag, 1)
            verdict = eng.value_load(bad_i[0:1, 0:1], min_val=0, max_val=P)
            with eng.If(verdict != 0):
                for i in range(2):
                    eng.wait_ge(s_out[i], 16 * NBATCH // 2)
                general()

        block = ctx.enter_context(nc.Block())

        @block.sync
        def _(sp):
            def load_row(n, first=False):
                for c in range(NC):
                    if not first:
                        sp.wait_ge(s_e, (n - 1) * NC + c + 1)
                        sp.wait_ge(s_half, (n - 1) * NC + c + 1)
                    src = adj_v[0, :, c * CH:(c + 1) * CH] if first else \
                        adj_v[bass.ds(n, 1), :, c * CH:(c + 1) * CH].rearrange("a p c -> (a p) c")
                    sp.dma_start(a_in[:, c, :], src).then_inc(s_in[c], 16)

            load_row(0, first=True)
            with sp.Fori(1, NB) as n:
                load_row(n)

            with sp.Fori(0, NBATCH // 2) as e2:
                for i in range(2):
                    e = e2 * 2 + i
                    sp.wait_ge(s_o, e + 1)
                    sp.dma_start(out_v[bass.ds(e, 1), :, :, :].rearrange("a p k f -> (a p) k f"),
                                 o_sb[:, i, :, :]).then_inc(s_out[i], 16)
            for i in range(2):
                sp.wait_ge(s_out[i], 16 * NBATCH // 2)

            def general_sp():
                sp.sem_inc(g_out, 16)
                for q in range(NC):
                    sp.dma_start(g_feat[:, q * CB:(q + 1) * CB, 0:F], x_v[:, q * CB:(q + 1) * CB, :]).then_inc(g_x, 16)
                for layer in range(2):
                    with sp.Fori(0, NB) as n:
                        for c in range(NC):
                            sp.wait_ge(g_tps, n * GQ + (layer * NB * GQ + 1))
                            sp.dma_start(a_in[:, c, :], adj_v[bass.ds(n, 1), :, c * CH:(c + 1) * CH]
                                         .rearrange("a p c -> (a p) c")).then_inc(g_in[c], 16)
                with sp.Fori(0, NBATCH) as e:
                    sp.wait_ge(g_o, e + 1)
                    sp.dma_start(out_v[bass.ds(e, 1), :, :, :].rearrange("a p k f -> (a p) k f"),
                                 o_sb[:, 0, :, :]).then_inc(g_out, 16)
                sp.wait_ge(g_out, 16 * NBATCH + 16)
            if_bad(sp, general_sp)

        @block.tensor
        def _(pe):
            def pack_chunk(n, c):
                this = count(pe, n * NC + c + 1)
                old = count(pe, (n - 1) * 2 + c // 2 + 1) if c % 2 == 0 and not (isinstance(n, int) and n == 0) else None
                settle(pe)
                pe.wait_ge(s_e, this)
                if old is not None:
                    pe.wait_ge(s_pk, old)
                for b in range(CB):
                    at = ((c % 2) * CB + b) * PK
                    last = nc.tensor.matmul(p_ps[c // 2][:, at:at + PK], e8[:, c, b * P:(b + 1) * P],
                                            pow_bf[:, :], start=True, stop=True)
                last.then_inc(s_pps, 1)

            def sum_quarter(q, n, k, i, first=False):
                if i % 2 == 0:
                    this = count(pe, n * 2 + (i // 2 + 1))
                    old = count(pe, n - 1) if i == 0 and not (isinstance(n, int) and n < 2) else None
                    settle(pe)
                    pe.wait_ge(s_t, this)
                    if old is not None:
                        pe.wait_ge(s_agg, old)
                if first:
                    of, value = ((s_xv, 1), (s_xp, 1), (s_xv, 2), (s_xv, 3))[i]
                    pe.wait_ge(of, value)
                for b in range(i * CB, (i + 1) * CB):
                    if b == 0:
                        nc.tensor.matmul(s_ps[k % 2][:, 0:SW], t_sb[:, b, :], x_all[:, 0:SW],
                                         start=True, stop=False)
                    if b < low(q):
                        nc.tensor.matmul(s_ps[k % 2][:, 0:HP], t_sb[:, b, :], h_parts[:, b, :],
                                         start=False, stop=False)
                    if b:
                        last = nc.tensor.matmul(s_ps[k % 2][:, HP:SW], t_sb[:, b, :], x_parts[:, b, 0:XW],
                                                start=False, stop=(b == NB - 1))
                if i % 2:
                    last.then_inc(s_sum, 1)

            def catch_up(q, n, k, part):
                if part == 0:
                    this = count(pe, n - (START[1] - 1))
                    settle(pe)
                    pe.wait_ge(s_u, this)
                    pe.wait_ge(s_uagg, this)
                w = width(q - 1)
                split = (piece(q) + 1) // 2
                for r in (range(split), range(split, piece(q)))[part]:
                    for b in range(w):
                        last = nc.tensor.matmul(u_ps[r // 4][:, (r % 4) * HP:(r % 4 + 1) * HP],
                                                u_sb[:, (r * w + b) * P:(r * w + b + 1) * P],
                                                h_parts[:, low(q - 1) + b, :], start=(b == 0), stop=(b == w - 1))
                    if r == piece(q) - 1:
                        last.then_inc(s_ups, 1)

            def transpose_cat(e):
                pe.wait_ge(s_feat, e + 1)
                pe.wait_ge(s_mean, e + 1)
                for k in range(BR):
                    last = nc.tensor.transpose(c_ps[:, k, :], cat[:, k, :], ident[:, :])
                last.then_inc(s_catps, 1)

            def dense_products(w, bias):
                for k in range(BR):
                    last = nc.tensor.matmul(z_ps[:, k * F:(k + 1) * F], cat_t[:, k, :], w[:, :],
                                            start=True, stop=not bias)
                    if bias:
                        last = nc.tensor.matmul(z_ps[:, k * F:(k + 1) * F], ones_f[0:1, :], b0_sb[0:1, :],
                                                start=False, stop=True)
                return last

            def dense(e, w, bias):
                pe.wait_ge(s_catt, e + 1)
                dense_products(w, bias).then_inc(s_zps, 1)

            def body(q, e, first=False):
                for k in range(BR):
                    n = e * BR + k
                    for c in range(NC):
                        pack_chunk(n, c)
                        if q and k == 0 and c == 0:
                            pe.wait_ge(s_h, low(q) // BR)
                        if not (first and k == 0):
                            sum_quarter(q, n - 1, (k - 1) % BR, c, first=first and k == 1)
                        if q and c < 2:
                            catch_up(q, n, k, c)
                        if not first and (k, c) == (1, 3):
                            transpose_cat(e - 1)
                        if not first and (k, c) == (2, 1):
                            dense(e - 1, w0_sb, False)

            def general_pe():
                for t in (g_tps, g_use, g_catps):
                    pe.sem_inc(t, 1)
                for layer in range(2):
                    w, bias = ((w0_sb, True), (w1_sb, False))[layer]

                    def transpose_group(n, g):
                        if g % (GQ // NC) == 0:
                            pe.wait_ge(g_in[g * NC // GQ], n * 16 + (layer * NB + 1) * 16)
                        if g >= 2:
                            pe.wait_ge(g_tsb, n * GQ + (layer * NB * GQ + g))
                        for b in range(BR):
                            col = (g * BR + b) * P
                            last = nc.tensor.transpose(tf_ps[g % 2][:, b, :],
                                                       a_in[:, col // CH, col % CH:col % CH + P], ident[:, :])
                        last.then_inc(g_tps, 1)

                    pe.wait_ge(g_ready, layer * NBATCH + 1)
                    with pe.Fori(0, NB) as n:
                        pe.wait_ge(g_tsb, n * GQ + (layer * NB * GQ + 1))
                        pe.wait_ge(g_took, n + (layer * NB + 1))
                        transpose_group(n, 0)
                        for g in range(GQ):
                            if g + 1 < GQ:
                                transpose_group(n, g + 1)
                            pe.wait_ge(g_tsb, n * GQ + (layer * NB * GQ + g + 2))
                            for b in range(BR):
                                last = nc.tensor.matmul(s_ps[0][:, 0:F + 1], g_t[:, g % 2, b, :],
                                                        g_feat[:, g * BR + b, :],
                                                        start=(g == 0 and b == 0), stop=(g == GQ - 1 and b == BR - 1))
                            last.then_inc(g_use, 1)
                    with pe.Fori(0, NBATCH) as e:
                        b = e + layer * NBATCH
                        pe.wait_ge(g_cat, b + 1)
                        for k in range(BR):
                            last = nc.tensor.transpose(c_ps[:, k, :], cat[:, k, :], ident[:, :])
                        last.then_inc(g_catps, 1)
                        pe.wait_ge(g_catt, b + 1)
                        dense_products(w, bias).then_inc(g_zps, 1)

            pe.sem_inc(s_ups, 1)
            pe.wait_ge(s_const, 1)
            pe.wait_ge(s_pow, 1)
            pe.wait_ge(s_w, 48)
            nc.tensor.transpose(c_ps[:, 0, 0:F], w1_raw[:, :], ident[0:F, 0:F]).then_inc(s_w1t, 1)
            for k in range(BR):
                last = nc.tensor.matmul(z_ps[:, k * F:(k + 1) * F], ones_f[0:1, :], b0_sb[0:1, :],
                                        start=True, stop=True)
            last.then_inc(s_w1t, 1)
            pe.wait_ge(s_w1, 2)
            body(0, 0, first=True)
            for q in range(NQ):
                e0, steps = batches(q)
                with pe.Fori(e0 + (q == 0), e0 + steps) as e:
                    body(q, e)
            for i in range(NC):
                sum_quarter(NQ - 1, NB - 1, BR - 1, i)

            def strip_sums(par, k, cols):
                bank = (u_ps, s_ps)[par][k // 2]
                for b in cols:
                    last = nc.tensor.matmul(bank[:, (k % 2) * HP:(k % 2 + 1) * HP],
                                            v_sb[:, par, k * last_w + b, :], h_parts[:, low(NQ - 1) + b, :],
                                            start=(b == 0), stop=(b == last_w - 1))
                return last

            def second(e, par):
                if e_in(e, 0, NBATCH - 1):
                    this = count(pe, e + 1)
                    old = count(pe, e * 2 - 2) if not (isinstance(e, int) and e < 2) else None
                    settle(pe)
                    pe.wait_ge(s_v, this)
                    if old is not None:
                        pe.wait_ge(s_vagg, old)
                for k in range(BR):
                    if e_in(e, 0, NBATCH - 1):
                        last = strip_sums(par, k, range(last_w))
                        if k % 2:
                            last.then_inc(s_vps, 1)
                    if k == 1 and e_in(e, 2, NBATCH + 1):
                        dense(e + NBATCH - 2, w1_sb, False)
                if e_in(e, 1, NBATCH):
                    transpose_cat(e + NBATCH - 1)

            known = last_w - BR
            pe.wait_ge(s_uagg, NB - START[1] + 1)
            pe.wait_ge(s_v, 1)
            pe.wait_ge(s_h, NBATCH - 1)
            for k in (0, 2):
                strip_sums(0, k, range(known))
            transpose_cat(NBATCH - 1)
            dense(NBATCH - 1, w0_sb, False)
            pe.wait_ge(s_bad, 1)
            nc.tensor.matmul(c_ps[0:1, 0, 0:1], bad[:, 1:2], ones_f[:, 0:1], start=True,
                             stop=True).then_inc(s_badps, 1)
            pe.wait_ge(s_h, NBATCH)
            for k in range(BR):
                last = strip_sums(0, k, range(known if k % 2 == 0 else 0, last_w))
                if k % 2:
                    last.then_inc(s_vps, 1)
            pe.wait_ge(s_agg, NB)
            in_steps(pe, second, first=1)
            if_bad(pe, general_pe)

        @block.scalar
        def _(act):
            act.dma_start(w0_sb[:, :], w0[:, :]).then_inc(s_w, 16)
            act.dma_start(w1_raw[:, :], w1[:, :]).then_inc(s_w, 16)
            act.dma_start(b0_sb[0:1, :], b0.unsqueeze(0)).then_inc(s_w, 16)
            for q in range(NC):
                act.dma_start(x_sb[:, q * CB:(q + 1) * CB, :], x_v[:, q * CB:(q + 1) * CB, :]).then_inc(s_x[q], 16)
            act.sem_inc(s_uagg, 1)

            halves = [a_in[:, c, :].bitcast(U16).rearrange("p (b two) -> p b two", two=2)[:, :, 1]
                      for c in range(NC)]

            def sum_halves(n, c):
                this = count(act, n * 16 + 16)
                old = count(act, n * NC + c - 1) if not (isinstance(n, int) and n * NC + c < 2) else None
                settle(act)
                act.wait_ge(s_in[c], this)
                if old is not None:
                    act.wait_ge(s_half, old)
                for i in range(HS):
                    ins = nc.scalar.activation(
                        junk[:, c % 2, i, :], halves[c][:, i * 1024:(i + 1) * 1024], ACT.Copy, scale=1.0 / 128,
                        accum_out=half_sum[:, bass.ds(n, 1), c * HS + i:c * HS + i + 1].rearrange("p a b -> p (a b)"))
                    if i == HS - 1:
                        ins.then_inc(s_half, 1)

            def take_packed(n, slot, h):
                act.wait_ge(s_pps, n * NC + 2 * h + 2)
                if not (isinstance(n, int) and n < 2):
                    act.wait_ge(s_t, n * 2 + (h - 3))
                    act.wait_ge(s_store, n - 1)
                nc.scalar.copy(pk[:, slot, h * 512:(h + 1) * 512], p_ps[h][:, :]).then_inc(s_pk, 1)

            def take_sums(n, e, slot, k, free):
                act.wait_ge(s_sum, n * 2 + 2)
                if k == 0 and free:
                    act.wait_ge(s_low, e - 1)
                    act.wait_ge(s_mean, e - 1)
                nc.scalar.copy(agg[:, slot, k, :], s_ps[k % 2][:, 0:SW]).then_inc(s_agg, 1)

            def take_catch_up(q, n):
                act.wait_ge(s_ups, n - (START[1] - 2))
                act.wait_ge(s_uadd, n - (START[1] - 1))
                for r in range(0, piece(q), 4):
                    rows = min(4, piece(q) - r)
                    ins = nc.scalar.copy(u_agg[:, r:r + rows, :].rearrange("p r f -> p (r f)"),
                                         u_ps[r // 4][:, 0:rows * HP])
                ins.then_inc(s_uagg, 1)

            def take_cat(e):
                act.wait_ge(s_catps, e + 1)
                if not (isinstance(e, int) and e == 0):
                    act.wait_ge(s_zps, e)
                nc.scalar.copy(cat_t[:, :, :].rearrange("p k i -> p (k i)"),
                               c_ps[:, :, :].rearrange("p k i -> p (k i)")).then_inc(s_catt, 1)

            def take_z(e, par):
                act.wait_ge(s_zps, e + (NBATCH + 1))
                if isinstance(e, int) and e < 2:
                    act.wait_ge(s_hn, NBATCH)
                else:
                    act.wait_ge(s_o, e - 1)
                nc.scalar.activation(y2[par].rearrange("p k i -> p (k i)"), z_ps[:, 0:BR * F],
                                     ACT.Copy, scale=1.0 / H_SCALE).then_inc(s_z, 1)

            def body(q, e, par, first=False):
                for k in range(BR):
                    n = e * BR + k
                    lead = first and k == 0
                    sum_halves(n, 0)
                    sum_halves(n, 1)
                    if not first and k == 2:
                        take_cat(e - 1)
                    sum_halves(n, 2)
                    if not lead:
                        take_packed(n - 1, (k - 1) % 2, 1)
                    if k > 1:
                        take_sums(n - 2, e, par, k - 2, not (isinstance(e, int) and e < 2))
                    elif not first:
                        take_sums(n - 2, e - 1, 1 - par, k + 2, False)
                    sum_halves(n, 3)
                    take_packed(n, k % 2, 0)
                    if q:
                        take_catch_up(q, n)

            def general_act():
                act.sem_inc(g_tsb, 1)
                for layer in range(2):
                    with act.Fori(0, NB) as n:
                        for g in range(GQ):
                            act.wait_ge(g_tps, n * GQ + (layer * NB * GQ + g + 2))
                            if g >= 2:
                                act.wait_ge(g_use, n * GQ + (layer * NB * GQ + g))
                            else:
                                act.wait_ge(g_use, n * GQ + (layer * NB * GQ + 1))
                            nc.scalar.copy(g_t[:, g % 2, :, :], tf_ps[g % 2]).then_inc(g_tsb, 1)
                    with act.Fori(0, NBATCH) as e:
                        b = e + layer * NBATCH
                        act.wait_ge(g_catps, b + 2)
                        nc.scalar.copy(cat_t[:, :, :], c_ps[:, :, :]).then_inc(g_catt, 1)
                        act.wait_ge(g_zps, b + 1)
                        nc.scalar.activation(z_sb[:, :, :].rearrange("p k i -> p (k i)"), z_ps[:, 0:BR * F],
                                             ACT.Copy if layer else ACT.Relu).then_inc(g_z, 1)

            act.wait_ge(s_w1t, 1)
            nc.scalar.copy(w1_sb[:, :], c_ps[:, 0, 0:F]).then_inc(s_w1, 1)
            act.wait_ge(s_w1t, 2)
            nc.scalar.copy(bias[:, :, :].rearrange("p k f -> p (k f)"), z_ps[:, 0:BR * F]).then_inc(s_w1, 1)
            for e in range(batches(0)[1]):
                body(0, e, e % 2, first=(e == 0))
            for q in range(1, NQ):
                e0, steps = batches(q)
                with act.Fori(e0 // 2, (e0 + steps) // 2) as e2:
                    for par in range(2):
                        body(q, e2 * 2 + par, par)
            take_packed(NB - 1, (NB - 1) % 2, 1)
            for k in range(BR - 2, BR):
                take_sums(NB - BR + k, NBATCH - 1, (NBATCH - 1) % 2, k, False)
            take_cat(NBATCH - 1)

            def second(e, par):
                for i in range(2):
                    if e_in(e, 2, NBATCH + 1):
                        if i == 0:
                            take_cat(e + NBATCH - 2)
                        else:
                            take_z(e - 2, par)
                    if e_in(e, 0, NBATCH - 1):
                        act.wait_ge(s_vps, e * 2 + i + 1)
                        if i == 0:
                            act.wait_ge(s_low, e + NBATCH - 1)
                            act.wait_ge(s_mean, e + NBATCH - 1)
                        nc.scalar.copy(agg[:, par, 2 * i:2 * i + 2, 0:HP],
                                       (u_ps, s_ps)[par][i][:, 0:2 * HP].rearrange("p (k f) -> p k f", k=2)
                                       ).then_inc(s_vagg, 1)

            in_steps(act, second)
            if_bad(act, general_act)

        MEAN1, FINISH1, FINISH2 = 5, 9, 5

        @block.vector
        def _(dve):
            link = Links(dve, s_dve, settle)
            bc = lambda t: t.unsqueeze(2).to_broadcast([P, BR, F])

            dve.wait_ge(s_const, 1)
            link(nc.vector.tensor_copy(pow_f[:, :], ident[:, P - PK:P]))
            for g in range(6, -1, -1):
                link(nc.vector.scalar_tensor_tensor(out=pow_f[:, :], in0=pow_f[:, :], scalar=2.0,
                                                    in1=ident[:, g * PK:(g + 1) * PK], op0=ALU.mult, op1=ALU.add))
            nc.vector.tensor_copy(pow_bf[:, :], pow_f[:, :]).then_inc(s_pow, 1)
            link(nc.vector.memset(x_parts[:, :, XP:XW], 1.0))
            link(nc.vector.memset(x_all[:, 0:HP], 0.0))

            def split_x(q, this):
                dve.wait_ge(s_x[q], 16)
                cols = slice(q * CB, (q + 1) * CB)
                hi, mid, lo = (x_parts[:, cols, i * F:(i + 1) * F] for i in range(3))
                link(nc.vector.tensor_copy(hi, x_sb[:, cols, :]))
                link(nc.vector.tensor_tensor(split_v, x_sb[:, cols, :], hi, ALU.subtract))
                link(nc.vector.tensor_copy(mid, split_v))
                nc.vector.tensor_tensor(lo, split_v, mid, ALU.subtract).then_inc(s_xv, 1)
                dve.wait_ge(s_xv, this)

            def center_w1():
                dve.wait_ge(s_w1, 1)
                link(nc.vector.tensor_tensor(w1_sb[0:F, :], w1_sb[0:F, :], ident[0:F, 0:F], ALU.add))
                link(nc.vector.tensor_reduce(small[:, 0, 0:1], w1_sb[:, :], AX_X, ALU.add))
                link(nc.vector.tensor_scalar(small[:, 0, 0:1], small[:, 0, 0:1], 1.0 / F, None, ALU.mult))
                link(nc.vector.tensor_tensor(w1_sb[:, :], w1_sb[:, :], small[:, 0, 0:1].to_broadcast([P, F]),
                                             ALU.subtract))

            def compare(n, c):
                t = n * NC + c
                this = count(dve, n * 16 + 16)
                old = count(dve, t - (NC - 1)) if not (isinstance(n, int) and n == 0) else None
                settle(dve)
                dve.wait_ge(s_in[c], this)
                if old is not None:
                    dve.wait_ge(s_pps, old)
                nc.vector.tensor_scalar(e8[:, c, :], a_in[:, c, :], 1.0, None, ALU.is_equal,
                                        saturate=False).then_inc(s_e, 1)

            def unpack_planes(dst, src):
                for g in range(8):
                    op, by = (ALU.logical_shift_left, 6 - g) if g < 7 else (ALU.logical_shift_right, 1)
                    ins = nc.vector.tensor_scalar(dst[:, :, g * PKW:(g + 1) * PKW], src, by, BIT4, op, ALU.bitwise_and)
                return ins

            def unpack(n, slot, h):
                packed = count(dve, n * 2 + (h + 1))
                old = count(dve, n * 2 + (h - 1)) if not (isinstance(n, int) and n == 0) else None
                settle(dve)
                dve.wait_ge(s_pk, packed)
                if old is not None:
                    dve.wait_ge(s_sum, old)
                half = slice(h * NB // 2, (h + 1) * NB // 2)
                unpack_planes(words(t_sb[:, half, :]),
                              pk_w[:, slot, :].rearrange("p (b w) -> p b w", w=PKW)[:, half, :]).then_inc(s_t, 1)

            def unpack_piece(q, n):
                w = width(q - 1)
                rows = count(dve, (n - (START[q] - 1)) * piece(q))
                old = count(dve, n - (START[1] - 1))
                settle(dve)
                dve.wait_ge(s_store, rows)
                dve.wait_ge(s_ups, old)
                unpack_planes(words(u_sb[:, 0:piece(q) * w * P].rearrange("p (b i) -> p b i", i=P)),
                              stored(q - 1, (n - START[q]) * piece(q), piece(q)).rearrange(
                                  "p (b w) -> p b w", w=PKW)).then_inc(s_u, 1)

            def mean1_steps(total, deg, rows, scale):
                link(nc.vector.tensor_scalar(degp1[:, bass.ds(rows, BR)], deg, scale, 1.0, ALU.mult, ALU.add))
                link(nc.vector.reciprocal(zdeg(rows), degp1[:, bass.ds(rows, BR)]))
                link(nc.vector.tensor_scalar(small[:, 1, :], degp1[:, bass.ds(rows, BR)], 1.0, None, ALU.max))
                link(nc.vector.reciprocal(small[:, 2, :], small[:, 1, :]))
                link(nc.vector.scalar_tensor_tensor(out=nsum[:, :, :], in0=total, scalar=scale,
                                                    in1=cat[:, :, 0:F], op0=ALU.mult, op1=ALU.add))
                return nc.vector.tensor_tensor(cat[:, :, F:2 * F], nsum[:, :, :], bc(small[:, 2, :]), ALU.mult)

            def mean1(e, par):
                this = count(dve, e + 1)
                settle(dve)
                dve.wait_ge(s_feat, this)
                dve.wait_ge(s_part, this)
                deg = agg[:, par, :, SW - 1:SW].rearrange("p k o -> p (k o)")
                mean1_steps(part_sum[:, :, :], deg, e * BR, 0.5).then_inc(s_mean, 1)

            def norms(done):
                link(nc.vector.scalar_tensor_tensor(out=sq_sb[:, :, :], in0=z_sb[:, :, :], scalar=0.0,
                                                    in1=z_sb[:, :, :], op0=ALU.max, op1=ALU.mult))
                link(nc.vector.tensor_reduce(small[:, 3, :], sq_sb[:, :, :], AX_X, ALU.add))
                nc.vector.tensor_scalar(small[:, 3, :], small[:, 3, :], 1e-24, None, ALU.max).then_inc(done, 1)

            def centre(src):
                link(nc.vector.tensor_reduce(small[:, 5, :], src, AX_X, ALU.add))
                link(nc.vector.tensor_scalar(small[:, 5, :], small[:, 5, :], 1.0 / F, None, ALU.mult))
                link(nc.vector.tensor_tensor(y_sb[:, :, :], src, bc(small[:, 5, :]), ALU.subtract))

            def variances(y, done, scale=1.0):
                link(nc.vector.tensor_tensor(sq_sb[:, :, :], y, y, ALU.mult))
                link(nc.vector.tensor_reduce(small[:, 6, :], sq_sb[:, :, :], AX_X, ALU.add))
                nc.vector.tensor_scalar(small[:, 6, :], small[:, 6, :], scale ** -2 / F, scale ** -2 * EPS,
                                        ALU.mult, ALU.add).then_inc(done, 1)

            def residual(root, value):
                dve.wait_ge(root, value)
                link(nc.vector.scalar_tensor_tensor(out=y_sb[:, :, :], in0=z_sb[:, :, :], scalar=0.0,
                                                    in1=bc(small[:, 4, :]), op0=ALU.max, op1=ALU.mult))
                link(nc.vector.tensor_tensor(y_sb[:, :, :], y_sb[:, :, :], cat[:, :, 0:F], ALU.add))
                centre(y_sb[:, :, :])

            def finish1(e, part):
                if part == 0:
                    if isinstance(e, int) and e == 0:
                        dve.wait_ge(s_w1, 2)
                    this = count(dve, e + 1)
                    settle(dve)
                    dve.wait_ge(s_zps, this)
                    link(nc.vector.tensor_tensor(z_sb[:, :, :], z_ps[:, 0:BR * F].rearrange("p (k f) -> p k f", f=F),
                                                 bias[:, :, :], ALU.add))
                    norms(s_var)
                if part == 1:
                    residual(s_root, e * 2 + 1)
                if part == 2:
                    variances(y_sb[:, :, :], s_var, H_SCALE)
                if part == 3:
                    dve.wait_ge(s_root, e * 2 + 2)
                    if not (isinstance(e, int) and e == 0):
                        dve.wait_ge(s_h, e)
                    nc.vector.tensor_tensor(hn_sb[:, :, :], y_sb[:, :, :], bc(small[:, 7, :]),
                                            ALU.mult).then_inc(s_hn, 1)

            def body(q, e, par, first=False):
                for k in range(BR):
                    n = e * BR + k
                    lead = first and k == 0
                    compare(n, 0)
                    if q:
                        unpack_piece(q, n)
                    if lead:
                        split_x(0, 1)
                    if not first and k == 3:
                        finish1(e - 1, 0)
                    compare(n, 1)
                    if not lead:
                        unpack(n - 1, (k - 1) % 2, 0)
                    if not first and k == 3:
                        finish1(e - 1, 1)
                    compare(n, 2)
                    if lead:
                        split_x(2, 2)
                    if not first and k == 3:
                        finish1(e - 1, 2)
                    compare(n, 3)
                    if lead:
                        split_x(3, 3)
                        center_w1()
                    else:
                        unpack(n - 1, (k - 1) % 2, 1)
                    if not first and k == 1:
                        mean1(e - 1, 1 - par)
                    if not first and k == 3:
                        finish1(e - 1, 3)

            body(0, 0, 0, first=True)
            for e in range(1, batches(0)[1]):
                body(0, e, e % 2)
            base = link.n
            for q in range(1, NQ):
                e0, steps = batches(q)
                with dve.Fori(0, steps // 2) as i2:
                    link.at(i2 * (2 * (MEAN1 + 1 + FINISH1)) + base)
                    for par in range(2):
                        body(q, i2 * 2 + (e0 + par), par)
                    assert link.n == 2 * (MEAN1 + 1 + FINISH1), link.n
                base += steps // 2 * link.n
            link.at(base)

            def unpack_last(e, par):
                if isinstance(e, int) and e == 0:
                    dve.wait_ge(s_half, NB * NC)
                    dve.wait_ge(s_e, NB * NC)
                    dve.wait_ge(s_store, NB)
                if not (isinstance(e, int) and e < 2):
                    old = count(dve, e * 2 - 2)
                    settle(dve)
                    dve.wait_ge(s_vps, old)
                unpack_planes(words(v_sb[:, par, :, :]),
                              stored(NQ - 1, e * BR, BR).rearrange("p (b w) -> p b w", w=PKW)).then_inc(s_v, 1)

            def mean2(e):
                this, old = count(dve, e + NBATCH + 1), count(dve, e + NBATCH)
                settle(dve)
                dve.wait_ge(s_low, this)
                dve.wait_ge(s_catps, old)
                nc.vector.scalar_tensor_tensor(out=cat[:, :, F:2 * F], in0=part_sum[:, :, :], scalar=0.5,
                                               in1=bc(zdeg(e * BR)), op0=ALU.mult,
                                               op1=ALU.mult).then_inc(s_mean, 1)

            def finish2_steps(dst, done, root, value):
                centre(z_sb[:, :, :])
                variances(y_sb[:, :, :], done)
                dve.wait_ge(root, value)
                return nc.vector.tensor_tensor(dst, y_sb[:, :, :], bc(small[:, 7, :]), ALU.mult)

            for h in range(2):
                unpack(NB - 1, (NB - 1) % 2, h)
            unpack_last(0, 0)
            unpack_last(1, 1)
            hs = half_sum[:, :, :].rearrange("p n j -> p (n j)")
            r_hs = e8[:, 0, :].bitcast(F32)[:, 0:NB * NC * HS]
            rows = e8[:, 1, :].bitcast(F32)
            dve.wait_ge(s_pps, NB * NC)
            link(nc.vector.tensor_scalar(r_hs, hs, ROUND, None, ALU.add))
            link(nc.vector.tensor_scalar(r_hs, r_hs, ROUND, None, ALU.subtract))
            link(nc.vector.tensor_tensor(r_hs, r_hs, hs, ALU.not_equal))
            link(nc.vector.tensor_reduce(bad[:, 0:1], r_hs, AX_X, ALU.max))
            link(nc.vector.tensor_reduce(rows[:, 0:NB], half_sum[:, :, :], AX_X, ALU.add))
            mean1(NBATCH - 1, 1)
            link(nc.vector.tensor_scalar(rows[:, NB:2 * NB], degp1[:, :], -1.0, 127.0, ALU.add, ALU.mult))
            link(nc.vector.tensor_tensor(rows[:, 0:NB], rows[:, 0:NB], rows[:, NB:2 * NB], ALU.not_equal))
            link(nc.vector.tensor_reduce(bad[:, 1:2], rows[:, 0:NB], AX_X, ALU.max))
            nc.vector.tensor_tensor(bad[:, 1:2], bad[:, 1:2], bad[:, 0:1], ALU.max).then_inc(s_bad, 1)
            for part in range(4):
                finish1(NBATCH - 1, part)
            dve.wait_ge(s_badps, 1)
            nc.vector.tensor_copy(bad_i[0:1, 0:1], c_ps[0:1, 0, 0:1]).then_inc(s_flag, 1)
            base += link.n
            link.at(base)

            def second(e, par):
                if e_in(e, 3, NBATCH + 2):
                    this = count(dve, e - 2)
                    old = count(dve, e + (2 * NBATCH - 3)) if e_in(e, 4, NBATCH + 2) else None
                    settle(dve)
                    dve.wait_ge(s_z, this)
                    if old is not None:
                        dve.wait_ge(s_root, old)
                    variances(y2[1 - par], s_var)
                if e_in(e, 1, NBATCH):
                    mean2(e - 1)
                if e_in(e, 1, NBATCH - 2):
                    unpack_last(e + 1, 1 - par)

            in_steps(dve, second, link, 2)
            base = link.base + link.n

            def general_dve():
                gb = base
                dve.sem_inc(g_took, 1)
                dve.wait_ge(g_x, 16 * NC)
                nc.vector.memset(g_feat[:, :, F:F + 1], 1.0).then_inc(g_ready, 1)
                for layer in range(2):
                    with dve.Fori(0, NB) as n:
                        this = count(dve, (n + (layer * NB + 1)) * GQ + 1)
                        settle(dve)
                        dve.wait_ge(g_use, this)
                        nc.vector.tensor_copy(g_agg[:, bass.ds(n, 1), :].rearrange("p a f -> p (a f)"),
                                              s_ps[0][:, 0:F + 1]).then_inc(g_took, 1)
                    dve.wait_ge(g_took, (layer + 1) * NB + 1)
                    with dve.Fori(0, NBATCH) as e:
                        b = e + layer * NBATCH
                        per = MEAN1 + FINISH1 if layer == 0 else FINISH2
                        link.at(e * (per + 1) + gb)
                        total = g_agg[:, bass.ds(e * BR, BR), 0:F]
                        deg = g_agg[:, bass.ds(e * BR, BR), F:F + 1].rearrange("p k o -> p (k o)")
                        feat = g_feat[:, bass.ds(e * BR, BR), 0:F]
                        old = count(dve, b + 1)
                        settle(dve)
                        dve.wait_ge(g_catps, old)
                        link(nc.vector.tensor_copy(cat[:, :, 0:F], feat))
                        if layer == 0:
                            mean1_steps(total, deg, e * BR, 1.0).then_inc(g_cat, 1)
                        else:
                            nc.vector.tensor_tensor(cat[:, :, F:2 * F], total, bc(zdeg(e * BR)),
                                                    ALU.mult).then_inc(g_cat, 1)
                        dve.wait_ge(g_z, b + 1)
                        if layer == 0:
                            norms(g_var)
                            residual(g_root, e * 2 + 1)
                            variances(y_sb[:, :, :], g_var)
                            this = count(dve, e * 2 + 2)
                            settle(dve)
                            dve.wait_ge(g_root, this)
                            nc.vector.tensor_tensor(feat, y_sb[:, :, :], bc(small[:, 7, :]),
                                                    ALU.mult).then_inc(g_ready, 1)
                        else:
                            dve.wait_ge(g_out, e * 16 + 16)
                            finish2_steps(o_sb[:, 0, :, :], g_var, g_root, e + (2 * NBATCH + 1)).then_inc(g_o, 1)
                        assert link.n == per + 1, link.n
                    gb += NBATCH * (per + 1)
            if_bad(dve, general_dve)

        FEATURES, SUMS, SPLIT, PIECE = 1, 2, 1, 1

        @block.gpsimd
        def _(pool):
            link = Links(pool, s_pool, settle)

            link(nc.gpsimd.memset(ones_f[:, :], 1.0))
            link(nc.gpsimd.memset(minus_half[:, :], -0.5))
            link(nc.gpsimd.memset(ident[:, :], 0.0))
            nc.gpsimd.affine_select(out=ident[:, :], in_=ident[:, :], compare_op=ALU.not_equal, fill=1.0,
                                    base=0, pattern=[[-1, P]], channel_multiplier=1).then_inc(s_const, 1)
            for q in range(1, NQ):
                w = width(q - 1) * PKW
                at = strip_base(q - 1) + (START[q] - 1) * w
                link(nc.gpsimd.memset(store[:, at:at + w], 0))

            def split_x(dst, src, tmp, done):
                link(nc.gpsimd.tensor_copy(dst[0], src))
                link(nc.gpsimd.tensor_tensor(tmp, src, dst[0], ALU.subtract))
                link(nc.gpsimd.tensor_copy(dst[1], tmp))
                nc.gpsimd.tensor_tensor(dst[2], tmp, dst[1], ALU.subtract).then_inc(done, 1)

            pool.wait_ge(s_x[1], 16)
            split_x([x_parts[:, CB:2 * CB, i * F:(i + 1) * F] for i in range(3)], x_sb[:, CB:2 * CB, :],
                    split_p, s_xp)
            pool.sem_inc(s_uadd, 1)

            def add_parts(dst, src, extra=None):
                ins = nc.gpsimd.tensor_tensor(dst, src[:, :, 0:F], src[:, :, F:2 * F], ALU.add)
                rest = [src[:, :, i * F:(i + 1) * F] for i in range(2, src.shape[2] // F)]
                for t in rest + ([extra] if extra is not None else []):
                    link(ins)
                    ins = nc.gpsimd.tensor_tensor(dst, dst, t, ALU.add)
                return ins

            def root(i, wait, value, done):
                pool.wait_ge(wait, value)
                src, dst = ((3, 4), (6, 7))[i]
                nc.gpsimd.tensor_tensor(small[:, dst, :], small[:, src, :], minus_half[:, :],
                                        ALU.pow).then_inc(done, 1)

            def keep(q, n, slot):
                this = count(pool, n * 2 + 2)
                settle(pool)
                pool.wait_ge(s_pk, this)
                for s in range(q, NQ):
                    ins = nc.gpsimd.tensor_copy(stored(s, n, 1), pk_w[:, slot, low(s) * PKW:low(s + 1) * PKW])
                ins.then_inc(s_store, 1)

            def add_piece(q, n):
                this = count(pool, n - (START[1] - 2))
                settle(pool)
                pool.wait_ge(s_uagg, this)
                rows = zone(lower, (n - START[q]) * piece(q), piece(q))
                sums = u_agg[:, 0:piece(q), 0:F]
                link(nc.gpsimd.tensor_tensor(sums, sums, u_agg[:, 0:piece(q), F:2 * F], ALU.add))
                nc.gpsimd.tensor_tensor(rows, rows, sums, ALU.add).then_inc(s_uadd, 1)

            def features(e, old_e, parts):
                if not (isinstance(old_e, int) and old_e == 0):
                    old = count(pool, old_e)
                    settle(pool)
                    pool.wait_ge(s_catps, old)
                    if parts is x_parts:
                        pool.wait_ge(s_hn, old)
                width_p = XP if parts is x_parts else HP
                add_parts(cat[:, :, 0:F], parts[:, bass.ds(e * BR, BR), 0:width_p]).then_inc(s_feat, 1)

            def batch_sums(e, par):
                rows = count(pool, (e + 1) * BR)
                old = count(pool, e) if not (isinstance(e, int) and e == 0) else None
                settle(pool)
                pool.wait_ge(s_agg, rows)
                if old is not None:
                    pool.wait_ge(s_mean, old)
                add_parts(part_sum[:, :, :], agg[:, par, :, HP:HP + XP]).then_inc(s_part, 1)
                link(add_parts(zone(lower, e * BR), agg[:, par, :, 0:HP]))
                pool.sem_inc(s_low, 1)

            def split_h(e):
                this = count(pool, e + 1)
                settle(pool)
                pool.wait_ge(s_hn, this)
                hi, lo = (h_parts[:, bass.ds(e * BR, BR), i * F:(i + 1) * F] for i in range(2))
                link(nc.gpsimd.tensor_copy(hi, hn_sb[:, :, :]))
                nc.gpsimd.tensor_tensor(lo, hn_sb[:, :, :], hi, ALU.subtract).then_inc(s_h, 1)

            def finish(e):
                root(0, s_var, e * 2 + 1, s_root)
                root(1, s_var, e * 2 + 2, s_root)

            def body(q, e, par, first=False):
                for k in range(BR):
                    n = e * BR + k
                    if not first and k == 3:
                        finish(e - 1)
                    if not first and k == 1:
                        features(e - 1, e - 1, x_parts)
                        batch_sums(e - 1, 1 - par)
                    if not (first and k == 0):
                        keep(q, n - 1, (k - 1) % 2)
                    if not first and k == 3:
                        split_h(e - 1)
                    if q:
                        add_piece(q, n)

            for e in range(batches(0)[1]):
                body(0, e, e % 2, first=(e == 0))
            base = link.n
            for q in range(1, NQ):
                e0, steps = batches(q)
                with pool.Fori(0, steps // 2) as i2:
                    links = 2 * (FEATURES + SUMS + SPLIT + BR * PIECE)
                    link.at(i2 * links + base)
                    for par in range(2):
                        body(q, i2 * 2 + (e0 + par), par)
                    assert link.n == links, link.n
                base += steps // 2 * links
            link.at(base)
            e = NBATCH - 1
            keep(NQ - 1, NB - 1, (NB - 1) % 2)
            features(e, e, x_parts)
            batch_sums(e, e % 2)
            finish(e)
            split_h(e)
            pool.wait_ge(s_h, NBATCH)

            def second_features(e):
                features(e, e + NBATCH, h_parts)

            def second_sums(e, par):
                rows, old = count(pool, e * 2 + 2), count(pool, e + NBATCH)
                settle(pool)
                pool.wait_ge(s_vagg, rows)
                pool.wait_ge(s_mean, old)
                add_parts(part_sum[:, :, :], agg[:, par, :, 0:HP], zone(lower, e * BR)).then_inc(s_low, 1)

            def second_norm(e, par):
                this = count(pool, e + (2 * NBATCH + 1))
                old = count(pool, (e - par) * 8) if not (isinstance(e, int) and e < 2) else None
                before = count(pool, e) if not (isinstance(e, int) and e == 0) else None
                settle(pool)
                if before is not None:
                    pool.wait_ge(s_o, before)
                root(1, s_var, this, s_root)
                pool.wait_ge(s_root, this)
                if old is not None:
                    pool.wait_ge(s_out[par], old)
                nc.gpsimd.tensor_tensor(o_sb[:, par, :, :], y2[par], small[:, 7, :].unsqueeze(2).to_broadcast(
                    [P, BR, F]), ALU.mult).then_inc(s_o, 1)

            def second(e, par):
                if e_in(e, 1, NBATCH):
                    second_sums(e - 1, 1 - par)
                if e_in(e, 3, NBATCH + 2):
                    second_norm(e - 3, 1 - par)
                if e_in(e, 0, NBATCH - 1):
                    second_features(e)

            base += link.n
            link.at(base)
            in_steps(pool, second, link, 1)

            def general_pool():
                with pool.Fori(0, NBATCH) as e:
                    root(0, g_var, e * 2 + 1, g_root)
                    root(1, g_var, e * 2 + 2, g_root)
                with pool.Fori(0, NBATCH) as e:
                    root(1, g_var, e + (2 * NBATCH + 1), g_root)
            if_bad(pool, general_pool)


def kernel(**inputs):
    import numpy as _np
    import concourse.bacc as _bacc
    from concourse import mybir as _mybir
    from concourse.bass_utils import run_bass_kernel_spmd as _run

    nc = _bacc.Bacc("TRN2", target_bir_lowering=False, num_devices=1)
    arrays, args = {}, []
    for name in ("x", "adj", "L0_gnn_W", "L0_gnn_b", "L1_gnn_W"):
        a = _np.ascontiguousarray(inputs[name])
        arrays[f"in_{name}"] = a
        args.append(nc.dram_tensor(f"in_{name}", a.shape, _mybir.dt.from_np(a.dtype), kind="ExternalInput").ap())
    res = nc.dram_tensor("out_h", (N, F), _mybir.dt.float32, kind="ExternalOutput").ap()
    gnn_kernel(nc, *args, res)
    r = _run(nc, [arrays], core_ids=[0])
    return r.results[0]["out_h"]
```
